# Optimizing a Trainium2 kernel written in Bass

```python
import numpy as np
import jax
import jax.numpy as jnp

def _softmax(x, axis=-1):
    return jax.nn.softmax(x, axis=axis)

def _gelu(x):
    return jax.nn.gelu(x, approximate=True)

def _silu(x):
    return jax.nn.silu(x)

def _sigmoid(x):
    return jax.nn.sigmoid(x)

def _layernorm(x, axis=-1, eps=1e-05):
    m = jnp.mean(x, axis=axis, keepdims=True)
    v = jnp.var(x, axis=axis, keepdims=True)
    return (x - m) / jnp.sqrt(v + eps)

def _scatter_add(tgt, idx, src, axis=0):
    return tgt.at[idx].add(src)

def _segment_sum(src, seg, n):
    return jax.ops.segment_sum(src, seg, n)
kernel_name = 'mk_prb_d2_jaxref_r8_03ef42'

def setup_inputs(seed: int=0):
    np.random.seed(seed)
    _w = jnp.asarray

    def _L0_attn_setup():
        import jax, jax.numpy as jnp
        import numpy as np
        D_IN = 128
        D_OUT = 128
        NUM_HEADS = 16
        HEAD_DIM = D_OUT // NUM_HEADS
        key = jax.random.key(seed)
        ks = jax.random.split(key, 6)
        s_in = 1.0 / np.sqrt(D_IN)
        s_out = 1.0 / np.sqrt(D_OUT)
        return {'x': jax.random.normal(ks[0], (2, 256, D_IN), dtype=jnp.float32), 'Wq': jax.random.uniform(ks[1], (D_OUT, D_IN), jnp.float32, -s_in, s_in), 'Wk': jax.random.uniform(ks[2], (D_OUT, D_IN), jnp.float32, -s_in, s_in), 'Wv': jax.random.uniform(ks[3], (D_OUT, D_IN), jnp.float32, -s_in, s_in), 'Wo': jax.random.uniform(ks[4], (D_OUT, D_OUT), jnp.float32, -s_out, s_out), 'bo': jax.random.uniform(ks[5], (D_OUT,), jnp.float32, -s_out, s_out)}
    _L0_attn_in = _L0_attn_setup()

    def _L0_ffn_setup():
        import jax, jax.numpy as jnp
        import numpy as np
        THRESHOLD = 0.1
        key = jax.random.key(seed)
        k1, k2, k3 = jax.random.split(key, 3)
        B, S, D, E = (4, 512, 128, 8)
        inputs = jax.random.normal(k1, (B, S, D), dtype=jnp.float32)
        gate_w = jax.random.normal(k2, (D, E), dtype=jnp.float32) * 0.02
        gate_b = jnp.zeros((E,), dtype=jnp.float32)
        expert_w = jax.random.normal(k3, (E, D, D), dtype=jnp.float32) * 0.02
        expert_b = jnp.zeros((E, D), dtype=jnp.float32)
        return {'inputs': inputs, 'gate_w': gate_w, 'gate_b': gate_b, 'expert_w': expert_w, 'expert_b': expert_b}
    _L0_ffn_in = _L0_ffn_setup()

    def _L1_attn_setup():
        import jax, jax.numpy as jnp
        import numpy as np
        D_MODEL = 128
        N_HEADS = 16
        D_HEAD = D_MODEL // N_HEADS
        B, T = (2, 256)
        EPS = 1e-05
        key = jax.random.key(seed)
        ks = jax.random.split(key, 5)
        s = 1.0 / np.sqrt(D_MODEL)
        return {'x': jax.random.normal(ks[0], (B, T, D_MODEL), dtype=jnp.float32), 'W_q': jax.random.normal(ks[1], (D_MODEL, D_MODEL), dtype=jnp.float32) * s, 'W_k': jax.random.normal(ks[2], (D_MODEL, D_MODEL), dtype=jnp.float32) * s, 'W_v': jax.random.normal(ks[3], (D_MODEL, D_MODEL), dtype=jnp.float32) * s, 'W_o': jax.random.normal(ks[4], (D_MODEL, D_MODEL), dtype=jnp.float32) * s, 'gn_weight': jnp.ones((D_MODEL,), dtype=jnp.float32), 'gn_bias': jnp.zeros((D_MODEL,), dtype=jnp.float32)}
    _L1_attn_in = _L1_attn_setup()

    def _L1_ffn_setup():
        import jax, jax.numpy as jnp
        import numpy as np
        DIM = 128
        HEADS = 16
        HD = DIM // HEADS
        M = 32
        E = 4
        K = 2
        HID = 256
        MID = 256
        LB = 0.01
        EPS = 1.1920929e-07

        def _rms(x, w):
            return x * jax.lax.rsqrt(jnp.mean(x * x, axis=-1, keepdims=True) + EPS) * w

        def _gelu(x):
            return jax.nn.gelu(x, approximate=False)
        key = jax.random.key(seed)
        ks = jax.random.split(key, 20)
        d = DIM
        w = lambda k, s: jax.random.normal(k, s, jnp.float32) * 0.02
        return {'x': jax.random.normal(ks[0], (4, 128, d), jnp.float32), 'n1_w': jnp.ones((d,), jnp.float32), 'n2_w': jnp.ones((d,), jnp.float32), 'wq': w(ks[1], (d, d)), 'wk': w(ks[2], (d, d)), 'wv': w(ks[3], (d, d)), 'wo': w(ks[4], (d, d)), 'qn_w': jnp.ones((HD,), jnp.float32), 'kn_w': jnp.ones((HD,), jnp.float32), 'gate_w': w(ks[5], (E, d)), 'e0_up': w(ks[6], (HID, d)), 'e0_down': w(ks[7], (d, HID)), 'e1_w1': w(ks[8], (HID, d)), 'e1_w2': w(ks[9], (HID, d)), 'e1_down': w(ks[10], (d, HID)), 'e2_l1': w(ks[11], (MID, d)), 'e2_l2': w(ks[12], (HID, MID)), 'e2_l3': w(ks[13], (MID, HID)), 'e2_l4': w(ks[14], (d, MID)), 'e3_down': w(ks[15], (d, d)), 'e3_up': w(ks[16], (HID, d)), 'e3_out': w(ks[17], (d, HID))}
    _L1_ffn_in = _L1_ffn_setup()
    _d = {'L0_attn_x': _L0_attn_in['x'], 'L0_attn_Wq': _L0_attn_in['Wq'], 'L0_attn_Wk': _L0_attn_in['Wk'], 'L0_attn_Wv': _L0_attn_in['Wv'], 'L0_attn_Wo': _L0_attn_in['Wo'], 'L0_attn_bo': _L0_attn_in['bo'], 'L0_ffn_gate_w': _L0_ffn_in['gate_w'], 'L0_ffn_gate_b': _L0_ffn_in['gate_b'], 'L0_ffn_expert_w': _L0_ffn_in['expert_w'], 'L0_ffn_expert_b': _L0_ffn_in['expert_b'], 'L1_attn_W_q': _L1_attn_in['W_q'], 'L1_attn_W_k': _L1_attn_in['W_k'], 'L1_attn_W_v': _L1_attn_in['W_v'], 'L1_attn_W_o': _L1_attn_in['W_o'], 'L1_attn_gn_weight': _L1_attn_in['gn_weight'], 'L1_attn_gn_bias': _L1_attn_in['gn_bias'], 'L1_ffn_n1_w': _L1_ffn_in['n1_w'], 'L1_ffn_n2_w': _L1_ffn_in['n2_w'], 'L1_ffn_wq': _L1_ffn_in['wq'], 'L1_ffn_wk': _L1_ffn_in['wk'], 'L1_ffn_wv': _L1_ffn_in['wv'], 'L1_ffn_wo': _L1_ffn_in['wo'], 'L1_ffn_qn_w': _L1_ffn_in['qn_w'], 'L1_ffn_kn_w': _L1_ffn_in['kn_w'], 'L1_ffn_gate_w': _L1_ffn_in['gate_w'], 'L1_ffn_e0_up': _L1_ffn_in['e0_up'], 'L1_ffn_e0_down': _L1_ffn_in['e0_down'], 'L1_ffn_e1_w1': _L1_ffn_in['e1_w1'], 'L1_ffn_e1_w2': _L1_ffn_in['e1_w2'], 'L1_ffn_e1_down': _L1_ffn_in['e1_down'], 'L1_ffn_e2_l1': _L1_ffn_in['e2_l1'], 'L1_ffn_e2_l2': _L1_ffn_in['e2_l2'], 'L1_ffn_e2_l3': _L1_ffn_in['e2_l3'], 'L1_ffn_e2_l4': _L1_ffn_in['e2_l4'], 'L1_ffn_e3_down': _L1_ffn_in['e3_down'], 'L1_ffn_e3_up': _L1_ffn_in['e3_up'], 'L1_ffn_e3_out': _L1_ffn_in['e3_out']}
    _x0 = _d['L0_attn_x']
    _d['L0_attn_x'] = jax.random.normal(jax.random.fold_in(jax.random.key(seed), 1), (4, 1024, 128), dtype=_x0.dtype)
    del _x0
    return _d

def reference(L0_attn_x, L0_attn_Wq, L0_attn_Wk, L0_attn_Wv, L0_attn_Wo, L0_attn_bo, L0_ffn_gate_w, L0_ffn_gate_b, L0_ffn_expert_w, L0_ffn_expert_b, L1_attn_W_q, L1_attn_W_k, L1_attn_W_v, L1_attn_W_o, L1_attn_gn_weight, L1_attn_gn_bias, L1_ffn_n1_w, L1_ffn_n2_w, L1_ffn_wq, L1_ffn_wk, L1_ffn_wv, L1_ffn_wo, L1_ffn_qn_w, L1_ffn_kn_w, L1_ffn_gate_w, L1_ffn_e0_up, L1_ffn_e0_down, L1_ffn_e1_w1, L1_ffn_e1_w2, L1_ffn_e1_down, L1_ffn_e2_l1, L1_ffn_e2_l2, L1_ffn_e2_l3, L1_ffn_e2_l4, L1_ffn_e3_down, L1_ffn_e3_up, L1_ffn_e3_out):

    def _L0_attn_ref(x, Wq, Wk, Wv, Wo, bo):
        import jax, jax.numpy as jnp
        import numpy as np
        D_IN = 128
        D_OUT = 128
        NUM_HEADS = 16
        HEAD_DIM = D_OUT // NUM_HEADS
        B, T, _ = x.shape
        H, Dh = (NUM_HEADS, HEAD_DIM)
        q = jnp.einsum('btd,ed->bte', x, Wq).reshape(B, T, H, Dh).transpose(0, 2, 1, 3)
        k = jnp.einsum('btd,ed->bte', x, Wk).reshape(B, T, H, Dh).transpose(0, 2, 1, 3)
        v = jnp.einsum('btd,ed->bte', x, Wv).reshape(B, T, H, Dh).transpose(0, 2, 1, 3)
        scores = jnp.einsum('bhqd,bhkd->bhqk', q, k) / jnp.sqrt(jnp.float32(Dh))
        causal = jnp.triu(jnp.ones((T, T), dtype=bool), k=1)
        scores = jnp.where(causal, -jnp.inf, scores)
        attn = jax.nn.softmax(scores, axis=-1)
        out = jnp.einsum('bhqk,bhkd->bhqd', attn, v)
        out = out.transpose(0, 2, 1, 3).reshape(B, T, H * Dh)
        return jnp.einsum('bte,oe->bto', out, Wo) + bo

    def _L0_ffn_ref(inputs, gate_w, gate_b, expert_w, expert_b):
        import jax, jax.numpy as jnp
        import numpy as np
        THRESHOLD = 0.1
        d = inputs.shape[-1]
        x = inputs.reshape(-1, d)
        gate_logits = jax.nn.softmax(x @ gate_w + gate_b, axis=-1)
        selected = (gate_logits >= THRESHOLD).astype(x.dtype)
        weights = gate_logits * selected
        wsum = jnp.sum(weights, axis=-1, keepdims=True)
        weights = weights / jnp.where(wsum == 0, jnp.ones_like(wsum), wsum)
        E = expert_w.shape[0]
        out = jnp.zeros((x.shape[0], expert_w.shape[-1]), dtype=x.dtype)
        for e in range(E):
            out = out + weights[:, e:e + 1] * (x @ expert_w[e] + expert_b[e])
        return out.reshape(*inputs.shape[:-1], out.shape[-1])

    def _L1_attn_ref(x, W_q, W_k, W_v, W_o, gn_weight, gn_bias):
        import jax, jax.numpy as jnp
        import numpy as np
        D_MODEL = 128
        N_HEADS = 16
        D_HEAD = D_MODEL // N_HEADS
        B, T = (2, 256)
        EPS = 1e-05
        b, t, dm = x.shape
        h, dh = (N_HEADS, D_HEAD)
        gammas = 1.0 - 2.0 ** (-5.0 - jnp.arange(h, dtype=jnp.float32))
        q = (x @ W_q.T).reshape(b, t, h, dh)
        k = (x @ W_k.T).reshape(b, t, h, dh)
        v = (x @ W_v.T).reshape(b, t, h, dh)
        idx = jnp.arange(t)
        diff = idx[:, None] - idx[None, :]
        pow_ = jnp.maximum(diff, 0).astype(jnp.float32)
        decay = jnp.where(diff >= 0, gammas[:, None, None] ** pow_, 0.0)
        scale = jnp.sqrt(jnp.float32(dh))
        attn = jnp.einsum('bihd,bjhd->bhij', q, k) * decay[None] / scale
        y = jnp.einsum('bhij,bjhd->bihd', attn, v)
        mean = y.mean(axis=(1, 3), keepdims=True)
        var = y.var(axis=(1, 3), keepdims=True)
        yn = (y - mean) / jnp.sqrt(var + EPS)
        yn = yn.reshape(b, t, dm) * gn_weight + gn_bias
        return yn @ W_o.T

    def _L1_ffn_ref(x, n1_w, n2_w, wq, wk, wv, wo, qn_w, kn_w, gate_w, e0_up, e0_down, e1_w1, e1_w2, e1_down, e2_l1, e2_l2, e2_l3, e2_l4, e3_down, e3_up, e3_out):
        import jax, jax.numpy as jnp
        import numpy as np
        DIM = 128
        HEADS = 16
        HD = DIM // HEADS
        M = 32
        E = 4
        K = 2
        HID = 256
        MID = 256
        LB = 0.01
        EPS = 1.1920929e-07

        def _rms(x, w):
            return x * jax.lax.rsqrt(jnp.mean(x * x, axis=-1, keepdims=True) + EPS) * w

        def _gelu(x):
            return jax.nn.gelu(x, approximate=False)
        B, T, C = x.shape
        h = _rms(x, n1_w)
        heads = lambda w_: (h @ w_.T).reshape(B, T, HEADS, HD).transpose(0, 2, 1, 3)
        q = _rms(heads(wq), qn_w)
        k = _rms(heads(wk), kn_w)
        v = heads(wv)
        scores = jnp.einsum('bhqd,bhkd->bhqk', q, k) * HD ** (-0.5)
        causal = jnp.tril(jnp.ones((T, T), bool))
        scores = jnp.where(causal[None, None], scores, -jnp.inf)
        attn = jax.nn.softmax(scores, axis=-1)
        ao = jnp.einsum('bhqk,bhkd->bhqd', attn, v).transpose(0, 2, 1, 3).reshape(B, T, C) @ wo.T
        ao = ao.at[:, :, :M].set(0.0)
        x = x + ao
        xf = _rms(x, n2_w).reshape(-1, C)
        N = xf.shape[0]
        logits = jnp.nan_to_num(xf @ gate_w.T)
        probs = jax.nn.softmax(logits, axis=-1)
        topv, topi = jax.lax.top_k(probs, K)
        topv = topv / (topv.sum(-1, keepdims=True) + 1e-08)
        wts = jnp.zeros((N, E), x.dtype).at[jnp.arange(N)[:, None], topi].add(topv)
        o0 = _gelu(xf @ e0_up.T) @ e0_down.T
        o1 = jax.nn.silu(xf @ e1_w1.T) * (xf @ e1_w2.T) @ e1_down.T
        o2 = _gelu(_gelu(_gelu(xf @ e2_l1.T) @ e2_l2.T) @ e2_l3.T) @ e2_l4.T
        o3 = _gelu(_gelu(xf @ e3_down.T) @ e3_up.T) @ e3_out.T
        moe = wts[:, 0:1] * o0 + wts[:, 1:2] * o1 + wts[:, 2:3] * o2 + wts[:, 3:4] * o3
        moe = moe.reshape(B, T, C).at[:, :, :M].set(0.0)
        return x + moe
    x = L0_attn_x
    xn = _layernorm(x, axis=-1)
    x = x + _L0_attn_ref(xn, L0_attn_Wq, L0_attn_Wk, L0_attn_Wv, L0_attn_Wo, L0_attn_bo) + _L0_ffn_ref(xn, L0_ffn_gate_w, L0_ffn_gate_b, L0_ffn_expert_w, L0_ffn_expert_b)
    xn = _layernorm(x, axis=-1)
    x = x + _L1_attn_ref(xn, L1_attn_W_q, L1_attn_W_k, L1_attn_W_v, L1_attn_W_o, L1_attn_gn_weight, L1_attn_gn_bias) + _L1_ffn_ref(xn, L1_ffn_n1_w, L1_ffn_n2_w, L1_ffn_wq, L1_ffn_wk, L1_ffn_wv, L1_ffn_wo, L1_ffn_qn_w, L1_ffn_kn_w, L1_ffn_gate_w, L1_ffn_e0_up, L1_ffn_e0_down, L1_ffn_e1_w1, L1_ffn_e1_w2, L1_ffn_e1_down, L1_ffn_e2_l1, L1_ffn_e2_l2, L1_ffn_e2_l3, L1_ffn_e2_l4, L1_ffn_e3_down, L1_ffn_e3_up, L1_ffn_e3_out)
    return x

_drawn_inputs = setup_inputs


def setup_inputs(seed=0):
    import zlib

    import numpy as np

    out = dict(_drawn_inputs(seed))
    spreads = {'L0_ffn_gate_b': (0.0, 0.1),
     'L0_ffn_expert_b': (0.0, 0.1),
     'L1_attn_gn_weight': (1.0, 0.2),
     'L1_attn_gn_bias': (0.0, 0.54),
     'L1_ffn_n1_w': (1.0, 0.6),
     'L1_ffn_n2_w': (1.0, 0.6),
     'L1_ffn_qn_w': (1.0, 0.6),
     'L1_ffn_kn_w': (1.0, 0.6)}
    factors = {'L0_attn_Wq': 3.803,
     'L0_attn_Wk': 3.698,
     'L1_ffn_wq': 8.0,
     'L1_ffn_wk': 8.0,
     'L1_ffn_wv': 8.0,
     'L1_ffn_wo': 8.0,
     'L1_ffn_gate_w': 8.0,
     'L1_ffn_e0_up': 8.0,
     'L1_ffn_e0_down': 8.0,
     'L1_ffn_e1_w1': 8.0,
     'L1_ffn_e1_w2': 8.0,
     'L1_ffn_e1_down': 8.0,
     'L1_ffn_e2_l1': 8.0,
     'L1_ffn_e2_l2': 8.0,
     'L1_ffn_e2_l3': 8.0,
     'L1_ffn_e2_l4': 8.0,
     'L1_ffn_e3_down': 8.0,
     'L1_ffn_e3_up': 8.0,
     'L1_ffn_e3_out': 8.0}
    for name, (base, spread) in spreads.items():
        noise = np.random.default_rng([zlib.crc32(name.encode()), seed]).standard_normal(out[name].shape)
        drawn = base * np.exp(spread * noise) if base else spread * noise
        out[name] = jnp.asarray(drawn.astype(out[name].dtype))
    for name, factor in factors.items():
        out[name] = (out[name] * factor).astype(out[name].dtype)
    return out
```

```python
from contextlib import ExitStack

import numpy as np

import concourse.bass as bass
from concourse import mybir

F32 = mybir.dt.float32
BF16 = mybir.dt.bfloat16
U8 = mybir.dt.uint8
ALU = mybir.AluOpType
ACT = mybir.ActivationFunctionType
AX_X = mybir.AxisListType.X

P = 128
D = 128
H = 16
DH = D // H
B = 4
T = 1024
NT = B * T // P
TB = T // P
CH = 512
TC = CH // P
NCH = B * T // CH
E0 = 8
E1 = 4
G = 4
NG = H // G
N = B * NG
HID = 256
MZ = 32
MW = D - MZ
NEG = -1e30
FMAX = float(np.finfo(np.float32).max)

WCOLS = [("a0_q", D), ("a0_k", D), ("a0_v", D), ("a0_o", D), ("f0_e", E0 * D), ("f0_gate", E0),
         ("a1_q", D), ("a1_kv", 2 * D), ("a1_k", D), ("a1_o", D),
         ("f1_qkv", 3 * D), ("f1_o", MW), ("f1_gate", E1),
         ("e0_up", HID), ("e0_dn", 2 * MW), ("e1_w1", HID), ("e1_w2", HID), ("e1_dn", 2 * MW),
         ("e2_l1", HID), ("e2_l2", 2 * HID), ("e2_l3", 2 * HID), ("e2_l4", 2 * MW),
         ("e3_dn", D), ("e3_up", HID), ("e3_out", 2 * MW)]
WAT = {}
_at = 0
for _n, _w in WCOLS:
    WAT[_n] = (_at, _w)
    _at += _w
NW = _at
COLS = ["gn_w", "gn_b", "n1_w", "n2_w", "qn_w", "kn_w", "g128"]
TABS = [("ident", P), ("mask", P), ("gq", P), ("gk", P), ("gktok", D), ("carry", D), ("bo", D), ("gate_b", E0), ("f0_b", D)]
TAT = {}
_at = 0
for _n, _w in TABS:
    TAT[_n] = (_at, _w)
    _at += _w
NTAB = _at

QT = [0, 0, 1, 1, 0, 2]
KT = [0, 1, 0, 1, 2, 0]
TERMS = len(QT)
ROWS = 64

EXP_STEPS = []
for _j in range(TB):
    if _j < 4:
        EXP_STEPS.append((_j, P * _j, CH - P * _j))
        EXP_STEPS.append((_j, CH, CH))
    else:
        EXP_STEPS.append((_j, P * _j, T - P * _j))
NE = len(EXP_STEPS)
DIAG = [k for k, (j, q0, w) in enumerate(EXP_STEPS) if q0 == P * j]
MAX_PIECES = []
for _i in range(TB):
    if _i < 4:
        MAX_PIECES.append((_i, 0, P * (_i + 1), _i, True))
    else:
        MAX_PIECES.append((_i, 0, CH, _i, False))
        MAX_PIECES.append((_i, CH, P * (_i + 1) - CH, TB + _i - 4, True))
NM = 2 * len(MAX_PIECES)
RING = NM + 1
AHEAD = 4


class Ctx:
    pass


def w_of(c, name):
    a, n = WAT[name]
    return c.w[:, a:a + n]


def tab(c, name):
    a, n = TAT[name]
    return c.tab[:, a:a + n]


def col(c, name):
    a = COLS.index(name)
    return c.cols[:, a:a + 1]


def stage_setup(nc, c):
    loaded = nc.alloc_semaphore("setup_loaded")
    cleared = nc.alloc_semaphore("setup_cleared")
    rows_set = nc.alloc_semaphore("setup_rows_set")
    with nc.sbuf_tensor("minus", [1, 4 * T], BF16) as minus, nc.Block() as block:
        @block.sync
        def _(sp):
            sp.dma_start(c.tab[:, :], c.in_tab).then_inc(loaded, 16)
            sp.dma_start(c.cols[:, :], c.in_cols).then_inc(loaded, 16)
            for k in range(NCH):
                src = c.in_x.rearrange("(t p) d -> p t d", p=P)
                sp.dma_start(c.x_all[:, k * TC:(k + 1) * TC, :], src[:, k * TC:(k + 1) * TC, :]).then_inc(loaded, 16)
            sp.wait_ge(loaded, 16 * (3 + NCH))

        @block.scalar
        def _(act):
            act.dma_start(c.w[:, :], c.in_w).then_inc(loaded, 16)

        @block.vector
        def _(dve):
            dve.memset(c.km[:, :, :], 0.0).then_inc(cleared, 1)
            dve.memset(c.qm[:, :, :], 0.0).then_inc(cleared, 1)
            dve.memset(c.ones[:, :], 1.0).then_inc(cleared, 1)
            dve.wait_ge(loaded, 16 * (3 + NCH))
            dve.tensor_copy(c.ident_bf[:, :], tab(c, "ident"))
            dve.tensor_copy(c.mask_bf[:, :], tab(c, "mask"))

        @block.gpsimd
        def _(pool):
            pool.memset(c.vst[:, :, :, :], 0.0).then_inc(cleared, 1)
            pool.memset(minus[:, :], -1.0).then_inc(cleared, 1)
            pool.memset(c.neghalf[:, :], -0.5)
            pool.wait_ge(cleared, 5)
            pool.memset(c.vst[:, :, :, DH:DH + 1], 1.0)
            for a in range(2):
                for t in range(2):
                    r = ROWS * a + 8 * t + TERMS
                    pool.dma_start(c.km[r:r + 1, :, :], minus[0:1, :].rearrange("p (s n) -> p s n", s=2)).then_inc(rows_set, 16)
            pool.wait_ge(rows_set, 64)


def stage_first(nc, c):
    ph = ExitStack()
    sb = lambda name, shape, dt=F32: ph.enter_context(nc.sbuf_tensor("p1_" + name, shape, dt))
    sem = lambda name: nc.alloc_semaphore("p1_" + name)
    stats = sb("stats", [P, 2, TC, 6])
    mv = sb("mv", [P, 2, TC, 2])
    var_eps = sb("var_eps", [P, 2, TC])
    rstd = sb("rstd", [P, 2, TC])
    xn = sb("xn", [P, 2, TC, D])
    xnT = sb("xnT", [P, 2, CH])
    parts = sb("parts", [P, 2, 2, 3, CH], BF16)
    rest = sb("rest", [P, 2, CH])
    lg = sb("lg", [P, TC, E0])
    ge = sb("ge", [P, TC, E0])
    wts = sb("wts", [P, TC, E0])
    mx = sb("mx", [P, 4, TC])
    wT = sb("wT", [E0, CH])
    mix = sb("mix", [P, TC, D])
    chain = sem("dve_chain")
    var_ready, rstd_ready, xn_ready = sem("var_ready"), sem("rstd_ready"), sem("xn_ready")
    pe_done = sem("pe_done")
    act_done = sem("act_done")
    rest_ready, parts_ready = sem("rest_ready"), sem("parts_ready")
    stored = [sem("stored0"), sem("stored1")]
    lg_taken, lg_ready, wts_ready = sem("lg_taken"), sem("lg_ready"), sem("wts_ready")
    base_ready, mixed = sem("base_ready"), sem("mixed")
    PE_T, PE_Q, PE_K, PE_V, PE_LG, PE_M0, PE_WT, PE_WB, PE_M1, NPE = range(10)
    A_XT, A_QH, A_KH, A_V, A_EXP, A_WT, NA = range(7)
    n_pe = lambda ch, k: ch * NPE + (k + 1)
    n_act = lambda ch, k: ch * NA + (k + 1) + 1
    bT, bQ, bK, bV = 0, 1, 2, 3

    with ph, nc.Block() as block:
        @block.vector
        def _(dve):
            with dve.Fori(0, NCH // 2) as i:
                for s in range(2):
                    ch = 2 * i + s
                    t0 = TB * i + TC * s
                    links = [0]

                    def link(ins):
                        links[0] += 1
                        ins.then_inc(chain, 1)
                        dve.wait_ge(chain, per * ch + links[0])

                    per = 11
                    fixed(dve)
                    for j in range(TC):
                        ins = dve.bn_stats(stats[:, s, j, :], c.x_all[:, bass.ds(t0 + j, 1), :])
                    link(ins)
                    fixed(dve)
                    for j in range(TC):
                        ins = dve.bn_aggr(mv[:, s, j, :], stats[:, s, j, :])
                    link(ins)
                    dve.tensor_scalar(var_eps[:, s, :], mv[:, s, :, 1], 1e-5, None, ALU.add).then_inc(var_ready, 1)
                    dve.wait_ge(rstd_ready, ch + 1)
                    for j in range(TC):
                        ins = dve.tensor_scalar(xn[:, s, j, :], c.x_all[:, bass.ds(t0 + j, 1), :], mv[:, s, j, 0:1],
                                                rstd[:, s, j:j + 1], ALU.subtract, ALU.mult)
                    ins.then_inc(xn_ready, 1)
                    for n, (a, bank) in enumerate(((A_QH, bQ), (A_KH, bK))):
                        dve.wait_ge(act_done, n_act(ch, a))
                        dve.wait_ge(parts_ready, 1 + 2 * ch + n)
                        dve.tensor_tensor(rest[:, n, :], c.ps[:, bank, :], parts[:, s, n, 0, :],
                                          ALU.subtract).then_inc(rest_ready, 1)
                    dve.wait_ge(pe_done, n_pe(ch, PE_LG))
                    gb = tab(c, "gate_b").unsqueeze(1).to_broadcast([P, TC, E0])
                    link(dve.tensor_tensor(lg[:, :, :], c.ps[:, bV, 0:TC * E0].rearrange("p (t e) -> p t e", e=E0), gb, ALU.add))
                    dve.tensor_reduce(mx[:, 0, :], lg[:, :, :], AX_X, ALU.max).then_inc(lg_taken, 1)
                    dve.wait_ge(lg_taken, ch + 1)
                    bc = lambda k: mx[:, k, :].unsqueeze(2).to_broadcast([P, TC, E0])
                    dve.tensor_tensor(lg[:, :, :], lg[:, :, :], bc(0), ALU.subtract).then_inc(lg_ready, 1)
                    dve.wait_ge(act_done, n_act(ch, A_EXP))
                    link(dve.tensor_reduce(mx[:, 1, :], ge[:, :, :], AX_X, ALU.add))
                    link(dve.reciprocal(mx[:, 2, :], mx[:, 1, :]))
                    link(dve.tensor_tensor(ge[:, :, :], ge[:, :, :], bc(2), ALU.mult))
                    link(dve.scalar_tensor_tensor(out=lg[:, :, :], in0=ge[:, :, :], scalar=0.1, in1=ge[:, :, :],
                                                  op0=ALU.is_ge, op1=ALU.mult))
                    link(dve.tensor_reduce(mx[:, 3, :], lg[:, :, :], AX_X, ALU.add))
                    link(dve.scalar_tensor_tensor(out=mx[:, 1, :], in0=mx[:, 3, :], scalar=0.0, in1=mx[:, 3, :],
                                                  op0=ALU.is_equal, op1=ALU.add))
                    link(dve.reciprocal(mx[:, 2, :], mx[:, 1, :]))
                    dve.tensor_tensor(wts[:, :, :], lg[:, :, :], bc(2), ALU.mult).then_inc(wts_ready, 1)
                    dve.wait_ge(pe_done, n_pe(ch, PE_WB))
                    dve.wait_ge(base_ready, ch + 1)
                    link(dve.tensor_tensor(mix[:, :, :], c.ps[:, bV, :].rearrange("p (t d) -> p t d", d=D),
                                           c.acc_all[:, bass.ds(t0, TC), :], ALU.add))
                    for half in range(2):
                        dve.wait_ge(pe_done, n_pe(ch, PE_M1 if half else PE_M0))
                        for e in range(E0):
                            for j in (2 * half, 2 * half + 1):
                                bank = 4 + 2 * (j % 2) + e // 4
                                last = e == E0 - 1
                                out = c.acc_all[:, bass.ds(t0 + j, 1), :] if last else mix[:, j:j + 1, :]
                                src = c.ps[:, bank, (e % 4) * D:(e % 4 + 1) * D].unsqueeze(1)
                                ins = dve.scalar_tensor_tensor(out=out, in0=src, scalar=wts[:, j, e:e + 1], in1=mix[:, j:j + 1, :],
                                                               op0=ALU.mult, op1=ALU.add)
                                ins.then_inc(mixed, 1)
                            dve.wait_ge(mixed, 1 + 32 * ch + 16 * half + 2 * e + 2)
                    assert links[0] == per, links

        @block.gpsimd
        def _(pool):
            for ahead in (act_done, parts_ready, rest_ready, mixed):
                pool.sem_inc(ahead, 1)
            for ahead in stored:
                pool.sem_inc(ahead, 16)
            with pool.Fori(0, NCH // 2) as i:
                for s in range(2):
                    ch = 2 * i + s
                    t0 = TB * i + TC * s
                    pool.wait_ge(var_ready, ch + 1)
                    pool.tensor_tensor(rstd[:, s, :], var_eps[:, s, :], c.neghalf[:, 0:TC], ALU.pow).then_inc(rstd_ready, 1)
                    bo = tab(c, "bo").unsqueeze(1).to_broadcast([P, TC, D])
                    pool.tensor_tensor(c.acc_all[:, bass.ds(t0, TC), :], c.x_all[:, bass.ds(t0, TC), :], bo,
                                       ALU.add).then_inc(base_ready, 1)
                    for n in range(2):
                        pool.wait_ge(rest_ready, 1 + 2 * ch + n + 1)
                        fixed(pool)
                        pool.tensor_copy(parts[:, s, n, 1, :], rest[:, n, :]).then_inc(c.pool_chain, 1)
                        pool.wait_ge(c.pool_chain, 2 * ch + n + 1)
                        pool.tensor_tensor(parts[:, s, n, 2, :], rest[:, n, :], parts[:, s, n, 1, :],
                                           ALU.subtract).then_inc(parts_ready, 1)

        @block.scalar
        def _(act):
            with act.Fori(0, NCH // 2) as i:
                for s in range(2):
                    ch = 2 * i + s
                    act.wait_ge(pe_done, n_pe(ch, PE_T))
                    act.activation(xnT[:, s, :], c.ps[:, bT, :], ACT.Copy).then_inc(act_done, 1)
                    for n, (k, bank) in enumerate(((PE_Q, bQ), (PE_K, bK))):
                        act.wait_ge(pe_done, n_pe(ch, k))
                        act.wait_ge(stored[s], 16 + 32 * i + 16 * n)
                        act.activation(parts[:, s, n, 0, :], c.ps[:, bank, :], ACT.Copy).then_inc(act_done, 1)
                    act.wait_ge(pe_done, n_pe(ch, PE_V))
                    dst = c.v_all[:, bass.ds(NG * i, NG), TC * s:TC * s + TC, :].rearrange("p g t d -> p t g d")
                    act.activation(dst, c.ps[:, bV, :].rearrange("p (t g d) -> p t g d", g=NG, d=G * DH),
                                   ACT.Copy).then_inc(act_done, 1)
                    act.wait_ge(lg_ready, ch + 1)
                    act.activation(ge[:, :, :], lg[:, :, :], ACT.Exp).then_inc(act_done, 1)
                    act.wait_ge(pe_done, n_pe(ch, PE_WT))
                    act.activation(wT[:, :], c.ps[0:E0, bT, :], ACT.Copy).then_inc(act_done, 1)

        @block.sync
        def _(sp):
            with sp.Fori(0, NCH // 2) as i:
                for s in range(2):
                    ch = 2 * i + s
                    for n, dst in enumerate((c.scr_q[0], c.scr_k[0])):
                        sp.wait_ge(parts_ready, 1 + 2 * ch + n + 1)
                        fixed(sp)
                        sp.dma_start(dst[:, :, bass.ds(ch * CH, CH)], parts[:, s, n, :, :]).then_inc(stored[s], 16)
            for s in range(2):
                sp.wait_ge(stored[s], 16 + 32 * (NCH // 2))

        @block.tensor
        def _(pe):
            with pe.Fori(0, NCH // 2) as i:
                for s in range(2):
                    ch = 2 * i + s
                    pe.wait_ge(xn_ready, ch + 1)
                    pe.wait_ge(act_done, 1 + ch * NA)
                    for j in range(TC):
                        ins = pe.transpose(c.ps[:, bT, j * P:(j + 1) * P], xn[:, s, j, :], tab(c, "ident"))
                    ins.then_inc(pe_done, 1)
                    pe.wait_ge(act_done, n_act(ch, A_XT))
                    pe.wait_ge(rest_ready, 1 + 2 * ch)
                    pe.matmul(c.ps[:, bQ, :], w_of(c, "a0_q"), xnT[:, s, :], start=True, stop=True).then_inc(pe_done, 1)
                    pe.matmul(c.ps[:, bK, :], w_of(c, "a0_k"), xnT[:, s, :], start=True, stop=True).then_inc(pe_done, 1)
                    pe.wait_ge(mixed, 1 + 32 * ch)
                    for j in range(TC):
                        ins = pe.matmul(c.ps[:, bV, j * D:(j + 1) * D], xnT[:, s, j * P:(j + 1) * P], w_of(c, "a0_v"),
                                        start=True, stop=True)
                    ins.then_inc(pe_done, 1)
                    pe.wait_ge(act_done, n_act(ch, A_V))
                    for j in range(TC):
                        ins = pe.matmul(c.ps[:, bV, j * E0:(j + 1) * E0], xnT[:, s, j * P:(j + 1) * P], w_of(c, "f0_gate"),
                                        start=True, stop=True)
                    ins.then_inc(pe_done, 1)

                    def experts(js):
                        for j in js:
                            for h in range(2):
                                ins = pe.matmul(c.ps[:, 4 + 2 * (j % 2) + h, :], xnT[:, s, j * P:(j + 1) * P],
                                                w_of(c, "f0_e")[:, h * 4 * D:(h + 1) * 4 * D], start=True, stop=True)
                        ins.then_inc(pe_done, 1)

                    experts((0, 1))
                    pe.wait_ge(wts_ready, ch + 1)
                    for j in range(TC):
                        ins = pe.transpose(c.ps[0:E0, bT, j * P:(j + 1) * P], wts[:, j, :], tab(c, "ident"))
                    ins.then_inc(pe_done, 1)
                    pe.wait_ge(act_done, n_act(ch, A_WT))
                    pe.wait_ge(lg_taken, ch + 1)
                    for j in range(TC):
                        ins = pe.matmul(c.ps[:, bV, j * D:(j + 1) * D], wT[:, j * P:(j + 1) * P], tab(c, "f0_b")[0:E0, :],
                                        start=True, stop=True)
                    ins.then_inc(pe_done, 1)
                    pe.wait_ge(mixed, 1 + 32 * ch + 16)
                    experts((2, 3))



def fixed(eng):
    eng.sem_inc(Ctx.passed, 1)


def stage_attention(nc, c, name, scr_q, scr_k, v_all, out_all):
    ph = ExitStack()
    sb = lambda nm, shape, dt=F32: ph.enter_context(nc.sbuf_tensor(name + nm, shape, dt))
    sem = lambda nm: nc.alloc_semaphore(name + nm)
    qe = sb("qe", [P, 2, 2 * T], BF16)
    ke = sb("ke", [P, 2, 2 * T], BF16)
    prob = sb("prob", [P, 4, G, CH])
    mx = sb("mx", [P, 2, 2, 2, TB + 4])
    mb = sb("mb", [P, 2, 2, 2, 2, TB], BF16)
    mT = sb("mT", [2 * 2 * 2 * TB, 2, P], BF16)
    oT = sb("oT", [P, T])
    rec = sb("rec", [P, TB, G])
    m_loaded = [sem("m_loaded0"), sem("m_loaded1")]
    e_copied = [sem("e_copied0"), sem("e_copied1")]
    e_rows = [sem("e_rows0"), sem("e_rows1")]
    s_filled, s_taken = sem("s_filled"), sem("s_taken")
    x_filled, x_taken = sem("x_filled"), sem("x_taken")
    masked = sem("masked")
    v_staged = sem("v_staged")
    pv_done = sem("pv_done")
    o_read, o_turned, o_taken = sem("o_read"), sem("o_turned"), sem("o_taken")
    max_link, m_split = sem("max_link"), sem("m_split")
    SB = lambda slot: 2 * slot
    XB, OB = 4, 6

    def rows_of(scr, t, pair, b, g):
        return scr[bass.ds(32 * g + 16 * pair, 16), t:t + 1, bass.ds(T * b, T)].rearrange("p o n -> p (o n)")

    with ph, nc.Block() as block:
        @block.sync
        def _(sp):
            def load(b, g, slot):
                for op, (dst, scr, which) in enumerate(((c.qm, scr_q, QT), (c.km, scr_k, KT))):
                    for t in range(TERMS):
                        for pair in range(2):
                            sp.dma_start(dst[t:t + 8 * 15 + 1:8, slot, T * pair:T * (pair + 1)],
                                         rows_of(scr, which[t], pair, b, g)).then_inc(m_loaded[slot], 16)

            def copies(n, i, slot):
                sp.wait_ge(m_loaded[slot], 16 * 4 * TERMS * (i + 1))
                fixed(sp)
                sp.wait_ge(pv_done, 1 + NE * n)
                sp.dma_start(qe[:, slot, :], c.qm[:, slot, :]).then_inc(e_copied[slot], 16)
                sp.dma_start(ke[:, slot, :], c.km[:, slot, :]).then_inc(e_copied[slot], 16)

            def max_rows(n, i, slot):
                sp.wait_ge(e_copied[slot], 32 * (i + 1))
                sp.wait_ge(s_taken, 2 + RING * (n + 1))
                for t in range(2):
                    for a in range(2):
                        r = ROWS * a + 8 * t + TERMS
                        k = 2 * TB * (2 * t + a)
                        sp.dma_start(qe[r:r + 1, slot, :].rearrange("o (c n) -> o c n", n=P),
                                     mT[k:k + 2 * TB, slot, :]).then_inc(e_rows[slot], 16)

            load(0, 0, 0)
            load(0, 1, 1)

            def batch(b, last):
                for g in range(NG):
                    n, i, s = NG * b + g, 2 * b + g // 2, g % 2
                    copies(n, i, s)
                    max_rows(n, i, s)
                    if g < 2 or not last:
                        sp.wait_ge(s_filled, RING * (n + 1))
                        fixed(sp)
                        load(b + g // 2, (g + 2) % NG, s)

            with sp.Fori(0, B - 1) as b:
                batch(b, False)
            batch(B - 1, True)
            for s in range(2):
                sp.wait_ge(e_rows[s], 16 * 4 * (N // 2))

        @block.gpsimd
        def _(pool):
            pool.sem_inc(s_taken, 2)
            pool.sem_inc(x_taken, 2)
            pool.sem_inc(pv_done, NE + 1)
            with pool.Fori(0, N // 2) as i:
                for s in range(2):
                    n = 2 * i + s
                    pool.wait_ge(pv_done, 1 + NE * n)
                    fixed(pool)
                    pool.tensor_copy(c.vst[:, s, :, 0:DH].rearrange("p (t h) d -> p t h d", h=G),
                                     v_all[:, bass.ds(n, 1), :, :].rearrange("p o t (h d) -> p (o t) h d", d=DH)).then_inc(v_staged, 1)
                    for k in DIAG:
                        pool.wait_ge(x_taken, 2 + 4 * NE * n + 4 * (k + 1))
                        fixed(pool)
                        blk = prob[:, k % 4, :, 0:P]
                        pool.affine_select(out=blk, in_=blk, compare_op=ALU.is_ge, fill=0.0, base=0,
                                           pattern=[[0, G], [1, P]], channel_multiplier=-1).then_inc(masked, 1)

        @block.scalar
        def _(act):
            def step(n, k, hh):
                w = EXP_STEPS[k][2]
                if hh == 0:
                    act.wait_ge(pv_done, 1 + NE * n + NE + k - 3)
                act.wait_ge(x_filled, 4 * NE * n + 4 * k + hh + 1)
                act.activation(prob[:, k % 4, hh, 0:w], c.ps[:, XB + hh % 2, 0:w], ACT.Exp, scale=DH ** -0.5).then_inc(x_taken, 1)

            def read_out(n):
                act.wait_ge(pv_done, 1 + NE * (n + 2))
                act.activation(oT[:, :].rearrange("p (b n) -> p b n", b=2), c.ps[:, OB:OB + 2, :], ACT.Copy).then_inc(o_read, 1)

            def group(n, before):
                for k in range(NE):
                    for hh in range(G):
                        step(n, k, hh)
                    if k == 1 and before:
                        read_out(n - 1)

            group(0, False)
            group(1, True)
            with act.Fori(1, N // 2) as i:
                for s in range(2):
                    group(2 * i + s, True)
            read_out(N - 1)

        @block.vector
        def _(dve):
            def maxima(n, s, before):
                for k in range(NM):
                    pair, (qi, k0, w, cl, _) = k // (NM // 2), MAX_PIECES[k % (NM // 2)]
                    dve.wait_ge(s_filled, RING * n + k + 1)
                    bank = SB((RING * s + k) % 2)
                    dve.tensor_reduce(mx[:, s, :, pair, cl], c.ps[:, bank:bank + 2, 0:w], AX_X, ALU.max).then_inc(s_taken, 1)
                    if k == AHEAD + 5 and before is not None:
                        normalise(before)
                dve.wait_ge(s_taken, 2 + RING * n + NM)
                flat = lambda a, b: mx[:, s, :, :, a:b]
                dve.tensor_tensor(flat(4, TB), flat(4, TB), flat(TB, TB + 4), ALU.max).then_inc(max_link, 1)
                dve.wait_ge(max_link, 2 * n + 1)
                dve.tensor_copy(mb[:, s, 0, :, :, :], flat(0, TB)).then_inc(max_link, 1)
                dve.wait_ge(max_link, 2 * n + 2)
                dve.tensor_tensor(mb[:, s, 1, :, :, :], flat(0, TB), mb[:, s, 0, :, :, :], ALU.subtract).then_inc(m_split, 1)
                dve.wait_ge(s_filled, RING * (n + 1))
                bank = SB((RING * s + NM) % 2)
                dve.tensor_copy(mT[:, s, :], c.ps[0:4 * 2 * TB, bank, 0:P // 2].bitcast(BF16)).then_inc(s_taken, 1)

            def normalise(n):
                dve.wait_ge(o_turned, n + 1)
                o = c.ps[:, OB:OB + 2, :].rearrange("p b (t h r) -> p (b t) h r", h=G, r=32)
                dve.reciprocal(rec[:, :, :], o[:, :, :, DH]).then_inc(c.norm_link, 1)
                dve.wait_ge(c.norm_link, c.norms + n + 1)
                dve.tensor_tensor(out_all[:, bass.ds(n, 1), :, :].rearrange("p o t (h d) -> p (o t) h d", d=DH), o[:, :, :, 0:DH],
                                  rec[:, :, :].unsqueeze(3).to_broadcast([P, TB, G, DH]), ALU.mult).then_inc(o_taken, 1)

            maxima(0, 0, None)
            maxima(1, 1, None)
            with dve.Fori(1, N // 2) as i:
                for s in range(2):
                    maxima(2 * i + s, s, 2 * i + s - 2)
            normalise(N - 2)
            normalise(N - 1)

        @block.tensor
        def _(pe):
            def max_piece(n, i, s, k):
                bank = SB((RING * s + k) % 2)
                if k == 0:
                    pe.wait_ge(m_loaded[s], 16 * 4 * TERMS * (i + 1))
                pe.wait_ge(s_taken, RING * n + k + 1)
                if k == NM:
                    pe.wait_ge(m_split, n + 1)
                    fixed(pe)
                    pe.transpose(c.ps[0:4 * 2 * TB, bank, 0:P // 2].bitcast(BF16),
                                 mb[:, s, :, :, :, :].rearrange("p t a c q -> p (t a c q)"), c.ident_bf[:, :]).then_inc(s_filled, 1)
                    return
                pair, (qi, k0, w, _, diag) = k // (NM // 2), MAX_PIECES[k % (NM // 2)]
                for a in range(2):
                    rows = slice(ROWS * a, ROWS * (a + 1))
                    at = T * pair
                    ins = pe.matmul(c.ps[:, bank + a, 0:w], c.qm[rows, s, at + P * qi:at + P * (qi + 1)],
                                    c.km[rows, s, at + k0:at + k0 + w], start=True, stop=not diag)
                if diag:
                    for a in range(2):
                        ins = pe.matmul(c.ps[:, bank + a, w - P:w], c.ident_bf[:, :], c.mask_bf[:, :], start=False, stop=True)
                ins.then_inc(s_filled, 1)

            def scores(n, i, s, k):
                j, q0, w = EXP_STEPS[k]
                if k == 0:
                    pe.wait_ge(e_rows[s], 16 * 4 * (i + 1))
                for hh in range(G):
                    pair, a = hh // 2, hh % 2
                    rows = slice(ROWS * a, ROWS * (a + 1))
                    at = T * pair
                    pe.wait_ge(x_taken, 4 * NE * n + 4 * k + hh + 1)
                    pe.matmul(c.ps[:, XB + a, 0:w], ke[rows, s, at + P * j:at + P * (j + 1)], qe[rows, s, at + q0:at + q0 + w],
                              start=True, stop=True).then_inc(x_filled, 1)

            def values(n, s, k):
                j, q0, w = EXP_STEPS[k]
                if k == 0:
                    pe.wait_ge(v_staged, n + 1)
                if k in DIAG:
                    pe.wait_ge(masked, len(DIAG) * n + DIAG.index(k) + 1)
                else:
                    pe.wait_ge(x_taken, 2 + 4 * NE * n + 4 * (k + 1))
                half = q0 // CH
                for hh in range(G):
                    ins = pe.matmul(c.ps[32 * hh:32 * hh + 32, OB + half, q0 - CH * half:q0 - CH * half + w],
                                    c.vst[:, s, G * j + hh, :], prob[:, k % 4, hh, 0:w],
                                    start=(j == 0), stop=(j == 4 * half + 3))
                ins.then_inc(pv_done, 1)

            def turn(n):
                pe.wait_ge(o_read, n + 1)
                for t in range(TB):
                    ins = pe.transpose(c.ps[:, OB + t // 4, P * (t % 4):P * (t % 4 + 1)], oT[:, P * t:P * (t + 1)], tab(c, "ident"))
                ins.then_inc(o_turned, 1)

            def group(n, i, s, first, ahead):
                todo = []
                if ahead >= 1:
                    todo += [(n + 1, i + s, 1 - s, k) for k in range(AHEAD, RING)]
                if ahead >= 2:
                    todo += [(n + 2, i + 1, s, k) for k in range(AHEAD)]
                for k in range(NE + 2):
                    if k < NE:
                        scores(n, i, s, k)
                        for _ in range(2 + (k == NE - 1)):
                            if todo:
                                max_piece(*todo.pop(0))
                    if k == 2 and not first:
                        turn(n - 1)
                        pe.wait_ge(o_taken, n)
                    if k >= 2:
                        values(n, s, k - 2)
                assert not todo

            for k in range(RING):
                max_piece(0, 0, 0, k)
            for k in range(AHEAD):
                max_piece(1, 0, 1, k)
            group(0, 0, 0, True, 2)
            group(1, 0, 1, False, 2)
            with pe.Fori(1, N // 2 - 1) as i:
                for s in range(2):
                    group(2 * i + s, i, s, False, 2)
            group(N - 2, N // 2 - 1, 0, False, 1)
            group(N - 1, N // 2 - 1, 1, False, 0)
            turn(N - 1)
    c.norms += N



def by_group(ap4, t, n):
    return ap4[:, :, t:t + n, :].rearrange("p g t d -> p t g d")


def stage_between(nc, c):
    ph = ExitStack()
    sb = lambda name, shape, dt=F32: ph.enter_context(nc.sbuf_tensor("p3_" + name, shape, dt))
    sem = lambda name: nc.alloc_semaphore("p3_" + name)
    aos, aoT = sb("aos", [P, TC, D]), sb("aoT", [P, CH])
    stats, mv = sb("stats", [P, TC, 6]), sb("mv", [P, TC, 2])
    var_eps, rstd = sb("var_eps", [P, TC]), sb("rstd", [P, TC])
    ms, r1 = sb("ms", [P, TC]), sb("r1", [P, TC])
    xn, xnT, hT = sb("xn", [P, TC, D]), sb("xnT", [P, CH]), sb("hT", [P, CH])
    rqk = sb("rqk", [P, 2, CH])
    ktok, vtok = sb("ktok", [P, TC, D]), sb("vtok", [P, TC, D])
    qk, sq = sb("qk", [P, TC, 2 * D]), sb("sq", [P, TC, 2 * D])
    hs = sb("hs", [P, TC * 2 * H])
    hr = sb("hr", [P, TC * 2 * H])
    state, step = sb("state", [P, D]), sb("step", [P, D])
    parts = sb("parts", [P, 2, 3, CH], BF16)
    rest = sb("rest", [P, 2, CH])
    chain, pool_chain, cleared = sem("dve_chain"), sem("pool_chain"), sem("cleared")
    PE = ["T_AO", "WO", "T_XN", "RQ", "RK", "KV", "F0", "F1", "F2", "F3", "U0", "U1", "U2", "U3", "TQ", "TK"]
    AC = ["AOT", "XNT", "XN1", "RQH", "RKH", "V", "VRET", "F0", "F1", "F2", "F3", "Y", "SQRT", "FQH", "FKH"]
    DV = ["X1", "VAR", "XN", "MS", "RQ", "RK", "RQR", "RKR", "KTOK", "S0", "S1", "S2", "S3", "HS", "QK", "FQR", "FKR"]
    PO = ["AO", "RSTD", "R1", "HT", "RQL", "RKL", "SQ", "FQL", "FKL"]
    pe_done, act_done, dve_done, pool_done = sem("pe_done"), sem("act_done"), sem("dve_done"), sem("pool_done")
    stored = [sem("stored0"), sem("stored1")]
    n_of = {id(pe_done): PE, id(act_done): AC, id(dve_done): DV, id(pool_done): PO}

    def at(done, ch, what):
        return 1 + len(n_of[id(done)]) * ch + n_of[id(done)].index(what) + 1

    with ph, nc.Block() as block:
        @block.gpsimd
        def _(pool):
            for ahead in (pe_done, act_done, dve_done, pool_done):
                pool.sem_inc(ahead, 1)
            for ahead in stored:
                pool.sem_inc(ahead, 16)
            with pool.Fori(0, NCH // 2) as i:
                for s in range(2):
                    ch, t0 = 2 * i + s, TB * i + TC * s

                    def low_parts(n, what, src):
                        pool.wait_ge(dve_done, at(dve_done, ch, src))
                        fixed(pool)
                        pool.tensor_copy(parts[:, n % 2, 1, :], rest[:, n % 2, :]).then_inc(pool_chain, 1)
                        pool.wait_ge(pool_chain, 4 * ch + n + 1)
                        pool.tensor_tensor(parts[:, n % 2, 2, :], rest[:, n % 2, :], parts[:, n % 2, 1, :],
                                           ALU.subtract).then_inc(pool_done, 1)

                    pool.wait_ge(pe_done, 1 + len(PE) * ch)
                    fixed(pool)
                    pool.tensor_copy(aos[:, :, :].rearrange("p t (g d) -> p t g d", g=NG),
                                     by_group(c.ao_all[:, bass.ds(NG * i, NG), :, :], TC * s, TC)).then_inc(pool_done, 1)
                    pool.wait_ge(dve_done, at(dve_done, ch, "VAR"))
                    pool.tensor_tensor(rstd[:, :], var_eps[:, :], c.neghalf[:, 0:TC], ALU.pow).then_inc(pool_done, 1)
                    pool.wait_ge(dve_done, at(dve_done, ch, "MS"))
                    pool.tensor_tensor(r1[:, :], ms[:, :], c.neghalf[:, 0:TC], ALU.pow).then_inc(pool_done, 1)
                    pool.wait_ge(act_done, at(act_done, ch, "XNT"))
                    fixed(pool)
                    pool.tensor_scalar(hT[:, :], xnT[:, :], col(c, "n1_w"), None, ALU.mult).then_inc(pool_done, 1)
                    low_parts(0, "RQL", "RQR")
                    low_parts(1, "RKL", "RKR")
                    pool.wait_ge(act_done, at(act_done, ch, "F3"))
                    pool.tensor_tensor(sq[:, :, :], qk[:, :, :], qk[:, :, :], ALU.mult).then_inc(pool_done, 1)
                    low_parts(2, "FQL", "FQR")
                    low_parts(3, "FKL", "FKR")

        @block.scalar
        def _(act):
            with act.Fori(0, NCH // 2) as i:
                for s in range(2):
                    ch, t0 = 2 * i + s, TB * i + TC * s

                    def high_part(n, src, done, what, scale):
                        act.wait_ge(done, at(done, ch, what))
                        act.wait_ge(stored[n % 2], 16 * (1 + 2 * ch + n // 2))
                        act.activation(parts[:, n % 2, 0, :], src, ACT.Copy, scale=scale).then_inc(act_done, 1)

                    act.wait_ge(pe_done, at(pe_done, ch, "T_AO"))
                    act.activation(aoT[:, :], c.ps[:, 0, :], ACT.Copy).then_inc(act_done, 1)
                    act.wait_ge(pe_done, at(pe_done, ch, "T_XN"))
                    act.activation(xnT[:, :], c.ps[:, 0, :], ACT.Copy).then_inc(act_done, 1)
                    act.activation(c.xn1_all[:, bass.ds(t0, TC), :], xn[:, :, :], ACT.Copy).then_inc(act_done, 1)
                    high_part(0, rqk[:, 0, :], dve_done, "RQ", 1.0)
                    high_part(1, rqk[:, 1, :], dve_done, "RK", 1.0)
                    act.wait_ge(pe_done, at(pe_done, ch, "KV"))
                    kv = c.ps[:, 4:6, :].rearrange("p b (t x d) -> p (b t) x d", x=2, d=D)
                    act.activation(vtok[:, :, :], kv[:, :, 1, :], ACT.Copy).then_inc(act_done, 1)
                    act.wait_ge(act_done, at(act_done, ch, "V"))
                    act.activation(by_group(c.vr_all[:, bass.ds(NG * i, NG), :, :], TC * s, TC),
                                   vtok[:, :, :].rearrange("p t (g d) -> p t g d", g=NG), ACT.Copy).then_inc(act_done, 1)
                    act.wait_ge(pool_done, at(pool_done, ch, "R1"))
                    for j in range(TC):
                        act.wait_ge(pe_done, at(pe_done, ch, f"F{j}"))
                        act.activation(qk[:, j, :], c.ps[:, 6 + j % 2, 0:2 * D], ACT.Copy, scale=r1[:, j:j + 1])
                        t = TC * s + j
                        act.activation(c.v_all[:, bass.ds(NG * i, NG), t:t + 1, :].rearrange("p g o d -> p (g o) d"),
                                       c.ps[:, 6 + j % 2, 2 * D:3 * D].rearrange("p (g d) -> p g d", g=NG), ACT.Copy,
                                       scale=r1[:, j:j + 1]).then_inc(act_done, 1)
                    act.wait_ge(pe_done, at(pe_done, ch, "U3"))
                    act.activation(by_group(c.y_all[:, bass.ds(NG * i, NG), :, :], TC * s, TC),
                                   c.ps[:, 2, :].rearrange("p (t g d) -> p t g d", t=TC, g=NG), ACT.Copy).then_inc(act_done, 1)
                    act.wait_ge(dve_done, at(dve_done, ch, "HS"))
                    act.activation(hr[:, :], hs[:, :], ACT.Sqrt).then_inc(act_done, 1)
                    high_part(2, c.ps[:, 0, :], pe_done, "TQ", col(c, "qn_w"))
                    high_part(3, c.ps[:, 1, :], pe_done, "TK", col(c, "kn_w"))

        @block.vector
        def _(dve):
            dve.memset(state[:, :], 0.0).then_inc(cleared, 1)
            dve.wait_ge(cleared, 1)
            with dve.Fori(0, NCH // 2) as i:
                for s in range(2):
                    ch, t0 = 2 * i + s, TB * i + TC * s
                    links = [0]
                    per = 2 + TC + TC

                    def link(ins):
                        links[0] += 1
                        ins.then_inc(chain, 1)
                        dve.wait_ge(chain, per * ch + links[0])

                    def left(n, src, what, scale):
                        dve.wait_ge(act_done, at(act_done, ch, what))
                        dve.wait_ge(pool_done, 1 + len(PO) * ch + (PO.index(("RQL", "RKL")[n % 2]) + 1 if n > 1 else 0))
                        dve.scalar_tensor_tensor(out=rest[:, n % 2, :], in0=src, scalar=scale, in1=parts[:, n % 2, 0, :],
                                                 op0=ALU.mult, op1=ALU.subtract).then_inc(dve_done, 1)

                    dve.wait_ge(pe_done, at(pe_done, ch, "WO"))
                    dve.tensor_tensor(c.x_all[:, bass.ds(t0, TC), :], c.ps[:, 1, :].rearrange("p (t d) -> p t d", d=D),
                                      c.acc_all[:, bass.ds(t0, TC), :], ALU.add).then_inc(dve_done, 1)
                    dve.wait_ge(dve_done, at(dve_done, ch, "X1"))
                    fixed(dve)
                    for j in range(TC):
                        ins = dve.bn_stats(stats[:, j, :], c.x_all[:, bass.ds(t0 + j, 1), :])
                    link(ins)
                    fixed(dve)
                    for j in range(TC):
                        ins = dve.bn_aggr(mv[:, j, :], stats[:, j, :])
                    link(ins)
                    dve.tensor_scalar(var_eps[:, :], mv[:, :, 1], 1e-5, None, ALU.add).then_inc(dve_done, 1)
                    dve.wait_ge(pool_done, at(pool_done, ch, "RSTD"))
                    for j in range(TC):
                        ins = dve.tensor_scalar(xn[:, j, :], c.x_all[:, bass.ds(t0 + j, 1), :], mv[:, j, 0:1],
                                                rstd[:, j:j + 1], ALU.subtract, ALU.mult)
                    ins.then_inc(dve_done, 1)
                    dve.wait_ge(dve_done, at(dve_done, ch, "XN"))
                    for j in range(TC):
                        ins = dve.tensor_tensor_reduce(out=step[:, :], in0=xn[:, j, :], in1=xn[:, j, :], scale=1.0, scalar=0.0,
                                                       op0=ALU.mult, op1=ALU.add, accum_out=ms[:, j:j + 1])
                        link(ins)
                    dve.tensor_scalar(ms[:, :], ms[:, :], 1.0 / D, 1.1920929e-07, ALU.mult, ALU.add).then_inc(dve_done, 1)
                    for n, (k, g) in enumerate((("RQ", "gq"), ("RK", "gk"))):
                        dve.wait_ge(pe_done, at(pe_done, ch, k))
                        dve.tensor_tensor(rqk[:, n, :].rearrange("p (t n) -> p t n", n=P),
                                          c.ps[:, 2 + n, :].rearrange("p (t n) -> p t n", n=P),
                                          tab(c, g).unsqueeze(1).to_broadcast([P, TC, P]), ALU.mult).then_inc(dve_done, 1)
                    left(0, rqk[:, 0, :], "RQH", 1.0)
                    left(1, rqk[:, 1, :], "RKH", 1.0)
                    dve.wait_ge(act_done, at(act_done, ch, "V"))
                    kv = c.ps[:, 4:6, :].rearrange("p b (t x d) -> p (b t) x d", x=2, d=D)
                    dve.tensor_tensor(ktok[:, :, :], kv[:, :, 0, :], tab(c, "gktok").unsqueeze(1).to_broadcast([P, TC, D]),
                                      ALU.mult).then_inc(dve_done, 1)
                    for j in range(TC):
                        dve.wait_ge(pe_done, at(pe_done, ch, f"U{j}"))
                        link(dve.tensor_tensor(step[:, :], c.ps[:, 3, j * D:(j + 1) * D], tab(c, "carry"), ALU.mult))
                        if s == 1 and j == TC - 1:
                            fixed(dve)
                            dve.memset(state[:, :], 0.0).then_inc(dve_done, 1)
                        else:
                            dve.scalar_tensor_tensor(out=state[:, :], in0=state[:, :], scalar=col(c, "g128"), in1=step[:, :],
                                                     op0=ALU.mult, op1=ALU.add).then_inc(dve_done, 1)
                    dve.wait_ge(pool_done, at(pool_done, ch, "SQ"))
                    dve.tensor_reduce(hr[:, :], sq[:, :, :].rearrange("p t (h d) -> p (t h) d", d=DH), AX_X,
                                      ALU.add).then_inc(c.hs_chain, 1)
                    dve.wait_ge(c.hs_chain, 2 * ch + 1)
                    dve.tensor_scalar(hr[:, :], hr[:, :], 1.0 / DH, 1.1920929e-07, ALU.mult, ALU.add).then_inc(c.hs_chain, 1)
                    dve.wait_ge(c.hs_chain, 2 * ch + 2)
                    dve.reciprocal(hs[:, :], hr[:, :]).then_inc(dve_done, 1)
                    dve.wait_ge(act_done, at(act_done, ch, "SQRT"))
                    heads = qk[:, :, :].rearrange("p t (h d) -> p (t h) d", d=DH)
                    dve.tensor_tensor(heads, heads, hr[:, :].unsqueeze(2).to_broadcast([P, TC * 2 * H, DH]),
                                      ALU.mult).then_inc(dve_done, 1)
                    left(2, c.ps[:, 0, :], "FQH", col(c, "qn_w"))
                    left(3, c.ps[:, 1, :], "FKH", col(c, "kn_w"))
                    assert links[0] == per

        @block.sync
        def _(sp):
            with sp.Fori(0, NCH // 2) as i:
                for s in range(2):
                    ch = 2 * i + s
                    for n, (dst, what) in enumerate(((c.scr_q[2], "RQL"), (c.scr_k[2], "RKL"), (c.scr_q[1], "FQL"), (c.scr_k[1], "FKL"))):
                        sp.wait_ge(pool_done, at(pool_done, ch, what))
                        fixed(sp)
                        sp.dma_start(dst[:, :, bass.ds(ch * CH, CH)], parts[:, n % 2, :, :]).then_inc(stored[n % 2], 16)
            for k in range(2):
                sp.wait_ge(stored[k], 16 * (1 + 2 * NCH))

        @block.tensor
        def _(pe):
            def each(fn):
                for j in range(TC):
                    ins = fn(j)
                ins.then_inc(pe_done, 1)

            tile = lambda j: slice(j * P, (j + 1) * P)
            ident = tab(c, "ident")
            with pe.Fori(0, NCH // 2) as i:
                for s in range(2):
                    ch = 2 * i + s
                    pe.wait_ge(pool_done, at(pool_done, ch, "AO"))
                    pe.wait_ge(dve_done, 1 + len(DV) * ch)
                    each(lambda j: pe.transpose(c.ps[:, 0, tile(j)], aos[:, j, :], ident))
                    pe.wait_ge(act_done, at(act_done, ch, "AOT"))
                    each(lambda j: pe.matmul(c.ps[:, 1, tile(j)], aoT[:, tile(j)], w_of(c, "a0_o"), start=True, stop=True))
                    pe.wait_ge(dve_done, at(dve_done, ch, "XN"))
                    each(lambda j: pe.transpose(c.ps[:, 0, tile(j)], xn[:, j, :], ident))
                    pe.wait_ge(act_done, at(act_done, ch, "XNT"))
                    pe.matmul(c.ps[:, 2, :], w_of(c, "a1_q"), xnT[:, :], start=True, stop=True).then_inc(pe_done, 1)
                    pe.matmul(c.ps[:, 3, :], w_of(c, "a1_k"), xnT[:, :], start=True, stop=True).then_inc(pe_done, 1)
                    each(lambda j: pe.matmul(c.ps[:, 4 + j // 2, 2 * D * (j % 2):2 * D * (j % 2 + 1)], xnT[:, tile(j)],
                                             w_of(c, "a1_kv"), start=True, stop=True))
                    pe.wait_ge(pool_done, at(pool_done, ch, "HT"))
                    for j in range(TC):
                        if j >= 2:
                            pe.wait_ge(act_done, at(act_done, ch, f"F{j - 2}"))
                        pe.matmul(c.ps[:, 6 + j % 2, 0:3 * D], hT[:, tile(j)], w_of(c, "f1_qkv"), start=True, stop=True).then_inc(pe_done, 1)
                    pe.wait_ge(dve_done, at(dve_done, ch, "KTOK"))
                    for j in range(TC):
                        if j:
                            pe.wait_ge(dve_done, at(dve_done, ch, f"S{j - 1}"))
                        pe.matmul(c.ps[:, 2, tile(j)], rqk[:, 0, tile(j)], state[:, :], start=True, stop=True)
                        pe.matmul(c.ps[:, 3, tile(j)], ktok[:, j, :], vtok[:, j, :], start=True, stop=True).then_inc(pe_done, 1)
                    pe.wait_ge(dve_done, at(dve_done, ch, "QK"))
                    for n in range(2):
                        each(lambda j: pe.transpose(c.ps[:, n, tile(j)], qk[:, j, n * D:(n + 1) * D], ident))
                    pe.wait_ge(act_done, 1 + len(AC) * (ch + 1))


def stage_retention(nc, c):
    ph = ExitStack()
    sb = lambda name, shape, dt=F32: ph.enter_context(nc.sbuf_tensor("r_" + name, shape, dt))
    sem = lambda name: nc.alloc_semaphore("r_" + name)
    sc = sb("sc", [P, 4, 2, 2, P])
    oT = sb("oT", [P, T])
    loaded = [sem("loaded0"), sem("loaded1")]
    filled, taken, masked = sem("filled"), sem("taken"), sem("masked")
    v_staged, pv_done = sem("v_staged"), sem("pv_done")
    o_read, o_turned, o_taken = sem("o_read"), sem("o_turned"), sem("o_taken")
    OB = 6

    with ph, nc.Block() as block:
        @block.sync
        def _(sp):
            with sp.Fori(0, B) as b:
                for g in range(NG):
                    n, slot = NG * b + g, g % 2
                    sp.wait_ge(pv_done, 1 + TB * n)
                    fixed(sp)
                    for dst, scr, which in ((c.qm, c.scr_q[2], QT), (c.km, c.scr_k[2], KT)):
                        for t in range(TERMS):
                            for pair in range(2):
                                r = 32 * g + 16 * pair
                                src = scr[r:r + 16, which[t]:which[t] + 1, bass.ds(T * b, T)].rearrange("p o n -> p (o n)")
                                sp.dma_start(dst[t:t + 8 * 15 + 1:8, slot, T * pair:T * (pair + 1)], src).then_inc(loaded[slot], 16)
            for s in range(2):
                sp.wait_ge(loaded[s], 16 * 4 * TERMS * (N // 2))

        @block.gpsimd
        def _(pool):
            pool.sem_inc(pv_done, TB + 1)
            pool.sem_inc(o_taken, 1)
            pool.sem_inc(taken, 2)
            with pool.Fori(0, N // 2) as i:
                for s in range(2):
                    n = 2 * i + s
                    pool.wait_ge(pv_done, 1 + TB * n)
                    fixed(pool)
                    pool.tensor_copy(c.vst[:, s, :, 0:DH].rearrange("p (t h) d -> p t h d", h=G),
                                     c.vr_all[:, bass.ds(n, 1), :, :].rearrange("p o t (h d) -> p (o t) h d", d=DH)).then_inc(v_staged, 1)
                    for t in range(TB):
                        pool.wait_ge(taken, 2 + TB * n + t + 1)
                        fixed(pool)
                        blk = sc[:, t % 4, :, :, :].rearrange("p a c n -> p (a c) n")
                        pool.affine_select(out=blk, in_=blk, compare_op=ALU.is_ge, fill=0.0, base=0,
                                           pattern=[[0, G], [1, P]], channel_multiplier=-1).then_inc(masked, 1)

        @block.scalar
        def _(act):
            def read_out(n):
                act.wait_ge(pv_done, 1 + TB * (n + 2))
                act.activation(oT[:, :].rearrange("p (b n) -> p b n", b=2), c.ps[:, OB:OB + 2, :], ACT.Copy).then_inc(o_read, 1)

            with act.Fori(0, N // 2) as i:
                for s in range(2):
                    n = 2 * i + s
                    for t in range(TB):
                        act.wait_ge(filled, TB * n + t + 1)
                        act.wait_ge(pv_done, 1 + TB * n + TB + t - 3)
                        bank = 2 * (t % 2)
                        act.activation(sc[:, t % 4, :, :, :], c.ps[:, bank:bank + 2, 0:2 * P].rearrange("p a (c n) -> p a c n", n=P),
                                       ACT.Copy).then_inc(taken, 1)
                    read_out(n)

        @block.vector
        def _(dve):
            with dve.Fori(0, N // 2) as i:
                for s in range(2):
                    n = 2 * i + s
                    dve.wait_ge(o_turned, n + 1)
                    o = c.ps[:, OB:OB + 2, :].rearrange("p b (t h r) -> p (b t) h r", h=G, r=32)
                    y = c.y_all[:, bass.ds(n, 1), :, :].rearrange("p o t (h d) -> p (o t) h d", d=DH)
                    dve.tensor_tensor(y, o[:, :, :, 0:DH], y, ALU.add).then_inc(o_taken, 1)

        @block.tensor
        def _(pe):
            with pe.Fori(0, N // 2) as i:
                for s in range(2):
                    n = 2 * i + s

                    def values(t):
                        if t == 0:
                            pe.wait_ge(v_staged, n + 1)
                            pe.wait_ge(o_taken, n + 1)
                        pe.wait_ge(masked, TB * n + t + 1)
                        for hh in range(G):
                            ins = pe.matmul(c.ps[32 * hh:32 * hh + 32, OB + t // 4, P * (t % 4):P * (t % 4 + 1)],
                                            c.vst[:, s, G * t + hh, :], sc[:, t % 4, hh % 2, hh // 2, :], start=True, stop=True)
                        ins.then_inc(pv_done, 1)

                    pe.wait_ge(loaded[s], 16 * 4 * TERMS * (i + 1))
                    for t in range(TB + 2):
                        if t < TB:
                            pe.wait_ge(taken, TB * n + t + 1)
                            for hh in range(G):
                                pair, a = hh // 2, hh % 2
                                rows = slice(ROWS * a, ROWS * (a + 1))
                                cols = slice(T * pair + P * t, T * pair + P * (t + 1))
                                ins = pe.matmul(c.ps[:, 2 * (t % 2) + a, P * pair:P * (pair + 1)], c.km[rows, s, cols],
                                                c.qm[rows, s, cols], start=True, stop=True)
                            ins.then_inc(filled, 1)
                        if t >= 2:
                            values(t - 2)
                    pe.wait_ge(o_read, n + 1)
                    for t in range(TB):
                        ins = pe.transpose(c.ps[:, OB + t // 4, P * (t % 4):P * (t % 4 + 1)], oT[:, P * t:P * (t + 1)], tab(c, "ident"))
                    ins.then_inc(o_turned, 1)


def stage_groupnorm(nc, c):
    ph = ExitStack()
    sb = lambda name, shape, dt=F32: ph.enter_context(nc.sbuf_tensor("g_" + name, shape, dt))
    sem = lambda name: nc.alloc_semaphore("g_" + name)
    sq = sb("sq", [P, NG, TB, G * DH])
    st = sb("st", [P, 4, H])
    sums, centred, squared, var_ready, rstd_ready, chain = (sem(n) for n in ("sums", "centred", "squared", "var_ready", "rstd_ready", "chain"))
    COUNT = float(T * DH)

    with ph, nc.Block() as block:
        @block.tensor
        def _(pe):
            with pe.Fori(0, B) as b:
                for k in range(2):
                    if k == 0:
                        pe.wait_ge(centred, 1 + 2 * b)
                    else:
                        pe.wait_ge(squared, b + 1)
                    for t in range(TB):
                        src = c.y_all[:, bass.ds(NG * b, NG), t:t + 1, :].rearrange("p g o d -> p (g o) d") if k == 0 else sq[:, :, t, :]
                        ins = pe.matmul(c.ps[:, k, 0:D], c.ones[:, :], src, start=(t == 0), stop=(t == TB - 1))
                    ins.then_inc(sums, 1)

        @block.vector
        def _(dve):
            with dve.Fori(0, B) as b:
                links = [0]

                def link(ins):
                    links[0] += 1
                    ins.then_inc(chain, 1)
                    dve.wait_ge(chain, 4 * b + links[0])

                def over_heads(k, op):
                    for g in range(NG):
                        y = c.y_all[:, bass.ds(NG * b + g, 1), :, :].rearrange("p o t (h d) -> p (o t) h d", d=DH)
                        v = st[:, k, G * g:G * (g + 1)].unsqueeze(1).unsqueeze(3).to_broadcast([P, TB, G, DH])
                        ins = dve.tensor_tensor(y, y, v, op)
                    ins.then_inc(centred, 1)

                dve.wait_ge(sums, 2 * b + 1)
                link(dve.tensor_reduce(st[:, 0, :], c.ps[:, 0, 0:D].rearrange("p (h d) -> p h d", d=DH), AX_X, ALU.add))
                link(dve.tensor_scalar(st[:, 1, :], st[:, 0, :], 1.0 / COUNT, None, ALU.mult))
                over_heads(1, ALU.subtract)
                dve.wait_ge(sums, 2 * b + 2)
                link(dve.tensor_reduce(st[:, 0, :], c.ps[:, 1, 0:D].rearrange("p (h d) -> p h d", d=DH), AX_X, ALU.add))
                link(dve.tensor_scalar(st[:, 2, :], st[:, 0, :], 1.0 / COUNT, 1e-5, ALU.mult, ALU.add))
                dve.tensor_copy(st[:, 0, :], st[:, 2, :]).then_inc(var_ready, 1)
                dve.wait_ge(rstd_ready, b + 1)
                over_heads(3, ALU.mult)

        @block.gpsimd
        def _(pool):
            pool.sem_inc(centred, 1)
            with pool.Fori(0, B) as b:
                pool.wait_ge(centred, 1 + 2 * b + 1)
                y = c.y_all[:, bass.ds(NG * b, NG), :, :]
                pool.tensor_tensor(sq[:, :, :, :], y, y, ALU.mult).then_inc(squared, 1)
                pool.wait_ge(var_ready, b + 1)
                pool.tensor_tensor(st[:, 3, :], st[:, 0, :], c.neghalf[:, 0:H], ALU.pow).then_inc(rstd_ready, 1)


def stage_after(nc, c):
    ph = ExitStack()
    sb = lambda name, shape, dt=F32: ph.enter_context(nc.sbuf_tensor("p6_" + name, shape, dt))
    sem = lambda name: nc.alloc_semaphore("p6_" + name)
    aos, aoT = sb("aos", [P, TC, D]), sb("aoT", [P, CH])
    ys, yT = sb("ys", [P, TC, D]), sb("yT", [P, CH])
    x2, x2n = sb("x2", [P, TC, D]), sb("x2n", [P, TC, D])
    base, junk = sb("base", [P, TC, D]), sb("junk", [P, D])
    ms, r2 = sb("ms", [P, TC]), sb("r2", [P, TC])
    xfT = sb("xfT", [P, CH])
    chain = sem("dve_chain")
    PE = ["T_AO", "T_Y", "WO", "RO", "T_XF", "GATE"]
    AC = ["AOT", "YT", "X2N", "XFT", "XFT_ALL"]
    DV = ["X2", "BASE", "MS", "LG"]
    PO = ["AO", "Y", "X2", "R2"]
    pe_done, act_done, dve_done, pool_done = sem("pe_done"), sem("act_done"), sem("dve_done"), sem("pool_done")
    n_of = {id(pe_done): PE, id(act_done): AC, id(dve_done): DV, id(pool_done): PO}

    def at(done, ch, what):
        return 1 + len(n_of[id(done)]) * ch + n_of[id(done)].index(what) + 1

    with ph, nc.Block() as block:
        @block.gpsimd
        def _(pool):
            for ahead in (pe_done, act_done, dve_done, pool_done):
                pool.sem_inc(ahead, 1)
            with pool.Fori(0, NCH // 2) as i:
                for s in range(2):
                    ch, t0 = 2 * i + s, TB * i + TC * s
                    pool.wait_ge(pe_done, 1 + len(PE) * ch)
                    fixed(pool)
                    for dst, src in ((aos, c.ao_all), (ys, c.y_all)):
                        pool.tensor_copy(dst[:, :, :].rearrange("p t (g d) -> p t g d", g=NG),
                                         by_group(src[:, bass.ds(NG * i, NG), :, :], TC * s, TC)).then_inc(pool_done, 1)
                    pool.wait_ge(dve_done, 1 + len(DV) * ch)
                    fixed(pool)
                    pool.tensor_copy(x2[:, :, 0:MZ], c.xn1_all[:, bass.ds(t0, TC), 0:MZ]).then_inc(pool_done, 1)
                    pool.wait_ge(dve_done, at(dve_done, ch, "MS"))
                    pool.tensor_tensor(r2[:, :], ms[:, :], c.neghalf[:, 0:TC], ALU.pow).then_inc(pool_done, 1)

        @block.scalar
        def _(act):
            with act.Fori(0, NCH // 2) as i:
                for s in range(2):
                    ch, t0 = 2 * i + s, TB * i + TC * s
                    act.wait_ge(pe_done, at(pe_done, ch, "T_AO"))
                    act.activation(aoT[:, :], c.ps[:, 0, :], ACT.Copy).then_inc(act_done, 1)
                    act.wait_ge(pe_done, at(pe_done, ch, "T_Y"))
                    act.activation(yT[:, :], c.ps[:, 1, :], ACT.Identity, scale=col(c, "gn_w"), bias=col(c, "gn_b")).then_inc(act_done, 1)
                    act.wait_ge(pool_done, at(pool_done, ch, "R2"))
                    for j in range(TC):
                        ins = act.activation(x2n[:, j, :], x2[:, j, :], ACT.Copy, scale=r2[:, j:j + 1])
                    ins.then_inc(act_done, 1)
                    act.wait_ge(pe_done, at(pe_done, ch, "T_XF"))
                    act.activation(xfT[:, :], c.ps[:, 4, :], ACT.Copy, scale=col(c, "n2_w")).then_inc(act_done, 1)
                    act.activation(c.xfT_all[:, bass.ds(ch * CH, CH)], c.ps[:, 4, :], ACT.Copy, scale=col(c, "n2_w")).then_inc(act_done, 1)

        @block.vector
        def _(dve):
            with dve.Fori(0, NCH // 2) as i:
                for s in range(2):
                    ch, t0 = 2 * i + s, TB * i + TC * s
                    per, links = 1 + TC, [0]

                    def link(ins):
                        links[0] += 1
                        ins.then_inc(chain, 1)
                        dve.wait_ge(chain, per * ch + links[0])

                    dve.wait_ge(pe_done, at(pe_done, ch, "WO"))
                    dve.wait_ge(act_done, 1 + len(AC) * ch)
                    dve.tensor_tensor(x2[:, :, MZ:D], c.ps[:, 2, :].rearrange("p (t d) -> p t d", d=D)[:, :, 0:MW],
                                      c.xn1_all[:, bass.ds(t0, TC), MZ:D], ALU.add).then_inc(dve_done, 1)
                    dve.wait_ge(pe_done, at(pe_done, ch, "RO"))
                    link(dve.tensor_tensor(base[:, :, :], c.ps[:, 3, :].rearrange("p (t d) -> p t d", d=D),
                                           c.x_all[:, bass.ds(t0, TC), :], ALU.add))
                    dve.wait_ge(dve_done, at(dve_done, ch, "X2"))
                    dve.wait_ge(pool_done, at(pool_done, ch, "X2"))
                    dve.tensor_tensor(c.x_all[:, bass.ds(t0, TC), :], base[:, :, :], x2[:, :, :], ALU.add).then_inc(dve_done, 1)
                    for j in range(TC):
                        link(dve.tensor_tensor_reduce(out=junk[:, :], in0=x2[:, j, :], in1=x2[:, j, :], scale=1.0, scalar=0.0,
                                                      op0=ALU.mult, op1=ALU.add, accum_out=ms[:, j:j + 1]))
                    dve.tensor_scalar(ms[:, :], ms[:, :], 1.0 / D, 1.1920929e-07, ALU.mult, ALU.add).then_inc(dve_done, 1)
                    dve.wait_ge(pe_done, at(pe_done, ch, "GATE"))
                    dve.tensor_copy(c.lg_all[:, bass.ds(t0, TC), :], c.ps[:, 5, 0:TC * E1].rearrange("p (t e) -> p t e", e=E1)).then_inc(dve_done, 1)

        @block.tensor
        def _(pe):
            def each(fn):
                for j in range(TC):
                    ins = fn(j)
                ins.then_inc(pe_done, 1)

            tile = lambda j: slice(j * P, (j + 1) * P)
            ident = tab(c, "ident")
            with pe.Fori(0, NCH // 2) as i:
                for s in range(2):
                    ch = 2 * i + s
                    pe.wait_ge(pool_done, at(pool_done, ch, "AO"))
                    each(lambda j: pe.transpose(c.ps[:, 0, tile(j)], aos[:, j, :], ident))
                    pe.wait_ge(pool_done, at(pool_done, ch, "Y"))
                    each(lambda j: pe.transpose(c.ps[:, 1, tile(j)], ys[:, j, :], ident))
                    pe.wait_ge(act_done, at(act_done, ch, "AOT"))
                    each(lambda j: pe.matmul(c.ps[:, 2, j * D:j * D + MW], aoT[:, tile(j)], w_of(c, "f1_o"), start=True, stop=True))
                    pe.wait_ge(act_done, at(act_done, ch, "YT"))
                    each(lambda j: pe.matmul(c.ps[:, 3, tile(j)], yT[:, tile(j)], w_of(c, "a1_o"), start=True, stop=True))
                    pe.wait_ge(act_done, at(act_done, ch, "X2N"))
                    each(lambda j: pe.transpose(c.ps[:, 4, tile(j)], x2n[:, j, :], ident))
                    pe.wait_ge(act_done, at(act_done, ch, "XFT"))
                    each(lambda j: pe.matmul(c.ps[:, 5, j * E1:(j + 1) * E1], xfT[:, tile(j)], w_of(c, "f1_gate"), start=True, stop=True))
                    pe.wait_ge(dve_done, 1 + len(DV) * (ch + 1))
                    pe.wait_ge(act_done, 1 + len(AC) * (ch + 1))


def stage_gate(nc, c):
    ph = ExitStack()
    sb = lambda name, shape, dt=F32: ph.enter_context(nc.sbuf_tensor("g1_" + name, shape, dt))
    sem = lambda name: nc.alloc_semaphore("g1_" + name)
    lg, ex, cnt, cmp, sel = (sb(n, [P, NT, E1]) for n in ("lg", "ex", "cnt", "cmp", "sel"))
    good = sb("good", [P, NT, E1], mybir.dt.uint32)
    red = sb("red", [P, NT])
    inv = sb("inv", [P, NT])
    chain, lg_ready, ex_ready = sem("chain"), sem("lg_ready"), sem("ex_ready")
    with ph, nc.Block() as block:
        @block.scalar
        def _(act):
            act.wait_ge(lg_ready, 1)
            act.activation(ex[:, :, :], lg[:, :, :], ACT.Exp).then_inc(ex_ready, 1)

        @block.vector
        def _(dve):
            links = [0]

            def link(ins):
                links[0] += 1
                ins.then_inc(chain, 1)
                dve.wait_ge(chain, links[0])

            wide = lambda a: a.unsqueeze(2).to_broadcast([P, NT, E1])
            link(dve.memset(lg[:, :, :], 0.0))
            link(dve.tensor_tensor(good[:, :, :], c.lg_all[:, :, :], c.lg_all[:, :, :], ALU.is_equal))
            link(dve.copy_predicated(lg[:, :, :], good[:, :, :], c.lg_all[:, :, :]))
            link(dve.tensor_scalar(lg[:, :, :], lg[:, :, :], FMAX, -FMAX, ALU.min, ALU.max))
            link(dve.tensor_reduce(red[:, :], lg[:, :, :], AX_X, ALU.max))
            dve.tensor_tensor(lg[:, :, :], lg[:, :, :], wide(red[:, :]), ALU.subtract).then_inc(lg_ready, 1)
            dve.wait_ge(ex_ready, 1)
            link(dve.tensor_reduce(red[:, :], ex[:, :, :], AX_X, ALU.add))
            link(dve.reciprocal(inv[:, :], red[:, :]))
            link(dve.tensor_tensor(ex[:, :, :], ex[:, :, :], wide(inv[:, :]), ALU.mult))
            link(dve.memset(cnt[:, :, :], 0.0))
            for f in range(E1):
                one = lambda a, b: ex[:, :, f:f + 1].to_broadcast([P, NT, b - a])
                if f + 1 < E1:
                    a, b = f + 1, E1
                    link(dve.tensor_tensor(cmp[:, :, a:b], one(a, b), ex[:, :, a:b], ALU.is_ge))
                    link(dve.tensor_tensor(cnt[:, :, a:b], cnt[:, :, a:b], cmp[:, :, a:b], ALU.add))
                if f:
                    a, b = 0, f
                    link(dve.tensor_tensor(cmp[:, :, a:b], one(a, b), ex[:, :, a:b], ALU.is_gt))
                    link(dve.tensor_tensor(cnt[:, :, a:b], cnt[:, :, a:b], cmp[:, :, a:b], ALU.add))
            link(dve.scalar_tensor_tensor(out=sel[:, :, :], in0=cnt[:, :, :], scalar=2.0, in1=ex[:, :, :],
                                          op0=ALU.is_lt, op1=ALU.mult))
            link(dve.tensor_reduce(red[:, :], sel[:, :, :], AX_X, ALU.add))
            link(dve.tensor_scalar(red[:, :], red[:, :], 1e-8, None, ALU.add))
            link(dve.reciprocal(inv[:, :], red[:, :]))
            link(dve.tensor_tensor(c.wts_all[:, :, :], sel[:, :, :], wide(inv[:, :]), ALU.mult))


def stage_experts(nc, c):
    ph = ExitStack()
    sb = lambda name, shape, dt=F32: ph.enter_context(nc.sbuf_tensor("e_" + name, shape, dt))
    sem = lambda name: nc.alloc_semaphore("e_" + name)
    UPS = [("e2_l1", None, "l1"), ("e3_dn", None, "d3"), ("e0_up", None, "u0"), ("e2_l2", "l1", "l2"), ("e3_up", "d3", "u3"),
           ("e1_w1", None, "a1"), ("e2_l3", "l2", "l3"), ("e1_w2", None, "b1")]
    DOWNS = [("e0_dn", "u0", 0), ("e3_out", "u3", 3), ("e2_l4", "l3", 2), ("e1_dn", "g1", 1)]
    units = []
    for w, src, dst in UPS:
        for half in range(WAT[w][1] // P // (2 if w in ("e2_l2", "e2_l3") else 1)):
            units.append((w, src, dst, half))
    NU = len(units)
    RB = 6
    hid = {n: sb(n, [P, k, CH]) for n, k in (("l1", 2), ("d3", 1), ("u0", 2), ("l2", 2), ("u3", 2), ("a1", 2), ("l3", 2), ("g1", 2))}
    th = sb("th", [P, 2, CH])
    wts = sb("wts", [P, 2, TC, E1])
    acc = sb("acc", [P, 2, TC, D])
    up_done, up_taken = sem("up_done"), sem("up_taken")
    gated = sem("gated")
    th_ready = sem("th_ready")
    dn_done, dn_taken = sem("dn_done"), sem("dn_taken")
    acc_ready = sem("acc_ready")
    written = [sem("written0"), sem("written1")]
    first_of = {}
    for u, (w, src, dst, half) in enumerate(units):
        first_of.setdefault(dst, u)
    width = {n: hid[n].shape[1] if n in hid else 2 for n in first_of}
    NA = NU - 2

    with ph, nc.Block() as block:
        @block.tensor
        def _(pe):
            with pe.Fori(0, NCH // 2) as i:
                for s in range(2):
                    ch = 2 * i + s
                    rhs_x = c.xfT_all[:, bass.ds(ch * CH, CH)]
                    pe.wait_ge(gated, 1 + 2 * ch)
                    pe.wait_ge(up_taken, 1 + NA * ch)
                    for u, (w, src, dst, half) in enumerate(units):
                        if u >= RB:
                            v = u - RB
                            pe.wait_ge(up_taken, 1 + NA * ch + v + 1)
                        kh = [0] if src is None else list(range(width[src]))
                        if src is not None:
                            pe.wait_ge(up_taken, 1 + NA * ch + first_of[src] + width[src])
                        for x in kh:
                            cols = w_of(c, w)[:, (x * HID if w in ("e2_l2", "e2_l3") else 0) + half * P:][:, 0:P]
                            ins = pe.matmul(c.ps[:, u % RB, :], cols, rhs_x if src is None else hid[src][:, x, :],
                                            start=(x == kh[0]), stop=(x == kh[-1]))
                        ins.then_inc(up_done, 1)
                    for k, (w, src, e) in enumerate(DOWNS):
                        if src == "g1":
                            pe.wait_ge(gated, 1 + 2 * ch + 2)
                        pe.wait_ge(dn_taken, 4 * ch + k + 1)
                        if src == "l3":
                            pe.wait_ge(up_taken, 1 + NA * (ch + 1))
                        elif src != "g1":
                            pe.wait_ge(up_taken, 1 + NA * ch + first_of[src] + width[src])
                        for j in range(TC):
                            for x in range(2):
                                ins = pe.matmul(c.ps[:, 6 + k % 2, j * D:j * D + MW], hid[src][:, x, j * P:(j + 1) * P],
                                                w_of(c, w)[:, x * MW:(x + 1) * MW], start=(x == 0), stop=(x == 1))
                        ins.then_inc(dn_done, 1)

        @block.scalar
        def _(act):
            with act.Fori(0, NCH // 2) as i:
                for s in range(2):
                    ch = 2 * i + s
                    act.wait_ge(dn_done, 1 + 4 * ch)
                    act.wait_ge(gated, 1 + 2 * ch)
                    for u, (w, src, dst, half) in enumerate(units[:NA]):
                        act.wait_ge(up_done, NU * ch + u + 1)
                        if dst == "a1":
                            act.activation(th[:, half, :], c.ps[:, u % RB, :], ACT.Tanh, scale=0.5).then_inc(th_ready, 1)
                            act.activation(hid["a1"][:, half, :], c.ps[:, u % RB, :], ACT.Copy, scale=0.5).then_inc(up_taken, 1)
                        else:
                            act.activation(hid[dst][:, half, :], c.ps[:, u % RB, :], ACT.Gelu).then_inc(up_taken, 1)

        @block.gpsimd
        def _(pool):
            pool.sem_inc(dn_taken, 2)
            for ahead in (gated, up_taken, dn_done):
                pool.sem_inc(ahead, 1)
            for ahead in written:
                pool.sem_inc(ahead, 16)
            with pool.Fori(0, NCH // 2) as i:
                for s in range(2):
                    ch, t0 = 2 * i + s, TB * i + TC * s
                    pool.wait_ge(written[s], 16 + 16 * i)
                    pool.wait_ge(dn_taken, 2 + 4 * ch)
                    fixed(pool)
                    pool.tensor_copy(acc[:, s, :, :], c.x_all[:, bass.ds(t0, TC), :])
                    pool.tensor_copy(wts[:, s, :, :], c.wts_all[:, bass.ds(t0, TC), :]).then_inc(acc_ready, 1)

        @block.vector
        def _(dve):
            with dve.Fori(0, NCH // 2) as i:
                for s in range(2):
                    ch = 2 * i + s
                    a1, g1 = hid["a1"], hid["g1"]
                    f = first_of["a1"]
                    dve.wait_ge(up_taken, 1 + NA * ch + f + 2)
                    for half in range(2):
                        dve.scalar_tensor_tensor(out=a1[:, half, :], in0=th[:, half, :], scalar=1.0, in1=a1[:, half, :],
                                                 op0=ALU.add, op1=ALU.mult).then_inc(c.silu, 1)
                    dve.wait_ge(dn_done, 1 + 4 * ch)
                    for half in range(2):
                        dve.wait_ge(c.silu, 2 * ch + half + 1)
                        dve.wait_ge(up_done, NU * (ch + 1) - 1 + half)
                        dve.tensor_tensor(g1[:, half, :], c.ps[:, (NA + half) % RB, :], a1[:, half, :], ALU.mult).then_inc(gated, 1)
                    dve.wait_ge(acc_ready, ch + 1)
                    for k, (w, src, e) in enumerate(DOWNS):
                        dve.wait_ge(dn_done, 1 + 4 * ch + k + 1)
                        if k:
                            dve.wait_ge(dn_taken, 2 + 4 * ch + k)
                        for j in range(TC):
                            ins = dve.scalar_tensor_tensor(out=acc[:, s, j, MZ:D], in0=c.ps[:, 6 + k % 2, j * D:j * D + MW],
                                                           scalar=wts[:, s, j, e:e + 1], in1=acc[:, s, j, MZ:D], op0=ALU.mult, op1=ALU.add)
                        ins.then_inc(dn_taken, 1)

        @block.sync
        def _(sp):
            with sp.Fori(0, NCH // 2) as i:
                for s in range(2):
                    ch, t0 = 2 * i + s, TB * i + TC * s
                    sp.wait_ge(dn_taken, 2 + 4 * (ch + 1))
                    fixed(sp)
                    sp.dma_start(c.out.rearrange("(t p) d -> p t d", p=P)[:, bass.ds(t0, TC), :], acc[:, s, :, :]).then_inc(written[s], 16)
            for s in range(2):
                sp.wait_ge(written[s], 16 + 16 * (NCH // 2))


def build(nc, x, w, cols, tabs, out, debug=None):
    c = Ctx()
    c.in_x, c.in_w, c.in_cols, c.in_tab, c.out = x, w, cols, tabs, out
    c.scr_q = [nc.dram_tensor(f"scratch_q{k}", (P, 3, B * T), BF16, kind="Internal").ap() for k in range(3)]
    c.scr_k = [nc.dram_tensor(f"scratch_k{k}", (P, 3, B * T), BF16, kind="Internal").ap() for k in range(3)]
    c.pool_chain = nc.alloc_semaphore("pool_chain")
    Ctx.passed = nc.alloc_semaphore("passed")
    c.norm_link = nc.alloc_semaphore("norm_link")
    c.norms = 0
    c.hs_chain = nc.alloc_semaphore("head_sums")
    c.silu = nc.alloc_semaphore("silu")
    with ExitStack() as ctx:
        sb = lambda name, shape, dt=F32: ctx.enter_context(nc.sbuf_tensor(name, shape, dt))
        c.w = sb("weights", [P, NW])
        c.cols = sb("columns", [P, len(COLS)])
        c.tab = sb("tables", [P, NTAB])
        c.x_all = sb("x_all", [P, NT, D])
        c.acc_all = sb("acc_all", [P, NT, D])
        c.v_all = sb("v_all", [P, N, TB, G * DH])
        c.ao_all = sb("ao_all", [P, N, TB, G * DH])
        c.xn1_all = c.acc_all
        c.vr_all = sb("vr_all", [P, N, TB, G * DH])
        c.y_all = sb("y_all", [P, N, TB, G * DH])
        c.xfT_all = c.v_all[:, :, :, :].rearrange("p n t d -> p (n t d)")
        c.lg_all = sb("lg_all", [P, NT, E1])
        c.wts_all = sb("wts_all", [P, NT, E1])
        c.ident_bf = sb("ident_bf", [P, P], BF16)
        c.mask_bf = sb("mask_bf", [P, P], BF16)
        c.ones = sb("ones", [P, P])
        c.neghalf = sb("neghalf", [P, P])
        c.qm = sb("qm", [P, 2, 2 * T], BF16)
        c.km = sb("km", [P, 2, 2 * T], BF16)
        c.vst = sb("vst", [P, 2, TB * G, 32])
        c.ps = ctx.enter_context(nc.psum_tensor("banks", [P, 8, CH], F32))
        stage_setup(nc, c)
        stage_first(nc, c)
        stage_attention(nc, c, "a0_", c.scr_q[0], c.scr_k[0], c.v_all, c.ao_all)
        stage_between(nc, c)
        stage_attention(nc, c, "a1_", c.scr_q[1], c.scr_k[1], c.v_all, c.ao_all)
        stage_retention(nc, c)
        stage_groupnorm(nc, c)
        stage_after(nc, c)
        stage_gate(nc, c)
        stage_experts(nc, c)
        if debug:
            debug(nc, c)


def layout(i):
    f = np.float32
    a = {k: np.asarray(v) for k, v in i.items()}
    t = lambda m: m.T
    two = lambda m: np.concatenate([m[:P], m[P:]], 1)
    L0, L1, F = "L0_attn_", "L1_attn_", "L1_ffn_"
    ws = {
        "a0_q": t(a[L0 + "Wq"]), "a0_k": t(a[L0 + "Wk"]), "a0_v": t(a[L0 + "Wv"]), "a0_o": t(a[L0 + "Wo"]),
        "f0_e": a["L0_ffn_expert_w"].transpose(1, 0, 2).reshape(D, E0 * D), "f0_gate": a["L0_ffn_gate_w"],
        "a1_q": t(a[L1 + "W_q"]), "a1_k": t(a[L1 + "W_k"]),
        "a1_kv": np.concatenate([t(a[L1 + "W_k"]), t(a[L1 + "W_v"])], 1), "a1_o": t(a[L1 + "W_o"]),
        "f1_qkv": np.concatenate([t(a[F + "wq"]), t(a[F + "wk"]), t(a[F + "wv"])], 1),
        "f1_o": t(a[F + "wo"])[:, MZ:], "f1_gate": t(a[F + "gate_w"]),
        "e0_up": t(a[F + "e0_up"]), "e0_dn": two(t(a[F + "e0_down"])[:, MZ:]),
        "e1_w1": t(a[F + "e1_w1"]), "e1_w2": t(a[F + "e1_w2"]), "e1_dn": two(t(a[F + "e1_down"])[:, MZ:]),
        "e2_l1": t(a[F + "e2_l1"]), "e2_l2": two(t(a[F + "e2_l2"])), "e2_l3": two(t(a[F + "e2_l3"])),
        "e2_l4": two(t(a[F + "e2_l4"])[:, MZ:]),
        "e3_dn": t(a[F + "e3_down"]), "e3_up": t(a[F + "e3_up"]), "e3_out": two(t(a[F + "e3_out"])[:, MZ:]),
    }
    w = np.concatenate([ws[n] for n, _ in WCOLS], 1)
    gam = np.repeat(1.0 - 2.0 ** (-5.0 - np.arange(H)), DH)
    pos = np.arange(P)
    cs = {"gn_w": a[L1 + "gn_weight"], "gn_b": a[L1 + "gn_bias"], "n1_w": a[F + "n1_w"], "n2_w": a[F + "n2_w"],
          "qn_w": np.tile(a[F + "qn_w"], H), "kn_w": np.tile(a[F + "kn_w"], H), "g128": (gam ** P).astype(f)}
    cols = np.stack([cs[n] for n in COLS], 1)
    same = (np.arange(D)[:, None] // DH) == (np.arange(D)[None, :] // DH)
    ts = {
        "ident": np.eye(P, dtype=f), "mask": np.triu(np.full((P, P), NEG, f), 1),
        "gq": (gam[:, None] ** pos[None] / np.sqrt(DH)).astype(f), "gk": (gam[:, None] ** -pos[None]).astype(f),
        "gktok": (gam[None] ** -pos[:, None]).astype(f), "carry": (same * (gam ** P)[:, None]).astype(f),
        "bo": np.repeat(a[L0 + "bo"][None], P, 0), "gate_b": np.repeat(a["L0_ffn_gate_b"][None], P, 0),
        "f0_b": np.concatenate([a["L0_ffn_expert_b"], np.zeros((P - E0, D), f)], 0),
    }
    tabs = np.concatenate([ts[n] for n, _ in TABS], 1)
    x = a["L0_attn_x"].reshape(B * T, D)
    return {"in_x": x, "in_w": w, "in_cols": cols, "in_tab": tabs}


def kernel(**inputs):
    from concourse import bacc
    from concourse.bass_utils import run_bass_kernel_spmd

    nc = bacc.Bacc("TRN2", target_bir_lowering=False, num_devices=1)
    arrays = {k: np.ascontiguousarray(v) for k, v in layout(inputs).items()}
    args = [nc.dram_tensor(k, v.shape, mybir.dt.from_np(v.dtype), kind="ExternalInput").ap() for k, v in arrays.items()]
    out = nc.dram_tensor("out_0", (B * T, D), F32, kind="ExternalOutput").ap()
    build(nc, *args, out)
    r = run_bass_kernel_spmd(nc, [arrays], core_ids=[0])
    return r.results[0]["out_0"].reshape(B, T, D)
```

```python
from contextlib import ExitStack

import numpy as np

import concourse.bass as bass
from concourse import mybir

F32 = mybir.dt.float32
BF16 = mybir.dt.bfloat16
U8 = mybir.dt.uint8
ALU = mybir.AluOpType
ACT = mybir.ActivationFunctionType
AX_X = mybir.AxisListType.X

P = 128
D = 128
H = 16
DH = D // H
B = 4
T = 1024
NT = B * T // P
TB = T // P
CH = 512
TC = CH // P
NCH = B * T // CH
E0 = 8
E1 = 4
G = 4
NG = H // G
N = B * NG
HID = 256
MZ = 32
MW = D - MZ
NEG = -1e30
FMAX = float(np.finfo(np.float32).max)

WCOLS = [("a0_q", D), ("a0_k", D), ("a0_v", D), ("a0_o", D), ("f0_e", E0 * D), ("f0_gate", E0),
         ("a1_q", D), ("a1_kv", 2 * D), ("a1_k", D), ("a1_o", D),
         ("f1_qkv", 3 * D), ("f1_o", MW), ("f1_gate", E1),
         ("e0_up", HID), ("e0_dn", 2 * MW), ("e1_w1", HID), ("e1_w2", HID), ("e1_dn", 2 * MW),
         ("e2_l1", HID), ("e2_l2", 2 * HID), ("e2_l3", 2 * HID), ("e2_l4", 2 * MW),
         ("e3_dn", D), ("e3_up", HID), ("e3_out", 2 * MW)]
WAT = {}
_at = 0
for _n, _w in WCOLS:
    WAT[_n] = (_at, _w)
    _at += _w
NW = _at
COLS = ["gn_w", "gn_b", "n1_w", "n2_w", "qn_w", "kn_w", "g128", *[f"head{k}" for k in range(2 * G)]]
TABS = [("ident", P), ("mask", P), ("gq", P), ("gk", P), ("gktok", D), ("carry", D), ("head_mean", D), ("tri", P), ("bo", D), ("gate_b", E0), ("f0_b", D)]
TAT = {}
_at = 0
for _n, _w in TABS:
    TAT[_n] = (_at, _w)
    _at += _w
NTAB = _at

QT = [0, 0, 1, 1, 0, 2]
KT = [0, 1, 0, 1, 2, 0]
TERMS = len(QT)
ROWS = 64

EXP_STEPS = []
for _j in range(TB):
    if _j < 4:
        EXP_STEPS.append((_j, P * _j, CH - P * _j))
        EXP_STEPS.append((_j, CH, CH))
    else:
        EXP_STEPS.append((_j, P * _j, T - P * _j))
NE = len(EXP_STEPS)
DIAG = [k for k, (j, q0, w) in enumerate(EXP_STEPS) if q0 == P * j]
MAX_PIECES = []
for _i in range(TB):
    if _i < 4:
        MAX_PIECES.append((_i, 0, P * (_i + 1), _i, True))
    else:
        MAX_PIECES.append((_i, 0, CH, _i, False))
        MAX_PIECES.append((_i, CH, P * (_i + 1) - CH, TB + _i - 4, True))
NM = 2 * len(MAX_PIECES)
AHEAD = 8
TURN_AT = 6
STEP_USES = [("piece", 1, k) for k in range(AHEAD, NM + 1)] + [("piece", 2, k) for k in range(AHEAD)]
STEP_USES.insert(TURN_AT, ("turn", -1, 0))
USES = len(STEP_USES)
PROLOGUE = NM + 1 + AHEAD
_total = sum(w for _, _, w in EXP_STEPS)
USE_STEP = [next(k for k in range(NE) if USES * sum(w for _, _, w in EXP_STEPS[:k + 1]) > u * _total) for u in range(USES)]


def ring_uses(n, i, s, first=False, follow=2):
    out = []
    for pos, (what, d, k) in enumerate(STEP_USES):
        if d <= follow and not (what == "turn" and first):
            at = PROLOGUE - 1 + pos + (first and pos < TURN_AT)
            if follow == 0:
                at = PROLOGUE - 1 - AHEAD
            turn_of_slot = i + (d == 2 or (d == 1 and s == 1)) if d > 0 else i
            out.append((what, n + d, turn_of_slot, (s + d) % 2, k, USES * n + at, 2 * (at % 2), USE_STEP[pos]))
    return out


def first_uses():
    return [("piece", g, 0, g, k, g * (NM + 1) + k, 2 * ((g * (NM + 1) + k) % 2), 0)
            for g, count in ((0, NM + 1), (1, AHEAD)) for k in range(count)]


def last_turn():
    at = PROLOGUE - AHEAD
    return ("turn", N - 1, 0, 1, 0, USES * (N - 1) + at, 2 * (at % 2), 0)


class Ctx:
    pass


def w_of(c, name):
    a, n = WAT[name]
    return c.w[:, a:a + n]


def tab(c, name):
    a, n = TAT[name]
    return c.tab[:, a:a + n]


def col(c, name):
    a = COLS.index(name)
    return c.cols[:, a:a + 1]


def stage_setup(nc, c):
    loaded = nc.alloc_semaphore("setup_loaded")
    cleared = nc.alloc_semaphore("setup_cleared")
    rows_set = nc.alloc_semaphore("setup_rows_set")
    with nc.sbuf_tensor("minus", [1, 4 * T], BF16) as minus, nc.Block() as block:
        @block.sync
        def _(sp):
            sp.dma_start(c.tab[:, :], c.in_tab).then_inc(loaded, 16)
            sp.dma_start(c.cols[:, :], c.in_cols).then_inc(loaded, 16)
            for k in range(NCH):
                src = c.in_x.rearrange("(t p) d -> p t d", p=P)
                sp.dma_start(c.x_all[:, k * TC:(k + 1) * TC, :], src[:, k * TC:(k + 1) * TC, :]).then_inc(loaded, 16)
            sp.wait_ge(loaded, 16 * (3 + NCH))

        @block.scalar
        def _(act):
            act.dma_start(c.w[:, :], c.in_w).then_inc(loaded, 16)

        @block.vector
        def _(dve):
            dve.memset(c.km[:, :, :], 0.0).then_inc(cleared, 1)
            dve.memset(c.qm[:, :, :], 0.0).then_inc(cleared, 1)
            dve.wait_ge(loaded, 16 * (3 + NCH))
            dve.tensor_copy(c.ident_bf[:, :], tab(c, "ident"))
            dve.tensor_copy(c.mask_bf[:, :], tab(c, "mask"))

        @block.gpsimd
        def _(pool):
            pool.memset(minus[:, :], -1.0).then_inc(cleared, 1)
            pool.memset(c.neghalf[:, :], -0.5)
            pool.wait_ge(cleared, 3)
            for a in range(2):
                for t in range(2):
                    r = ROWS * a + 8 * t + TERMS
                    pool.dma_start(c.km[r:r + 1, :, :], minus[0:1, :].rearrange("p (s n) -> p s n", s=2)).then_inc(rows_set, 16)
            pool.wait_ge(rows_set, 64)


def stage_first(nc, c):
    ph = ExitStack()
    sb = lambda name, shape, dt=F32: ph.enter_context(nc.sbuf_tensor("p1_" + name, shape, dt))
    sem = lambda name: nc.alloc_semaphore("p1_" + name)
    stats = sb("stats", [P, 2, TC, 6])
    mv = sb("mv", [P, 2, TC, 2])
    var_eps = sb("var_eps", [P, 2, TC])
    rstd = sb("rstd", [P, 2, TC])
    xn = sb("xn", [P, 2, TC, D])
    xnT = sb("xnT", [P, 2, CH])
    parts = sb("parts", [P, 2, 2, 3, CH], BF16)
    rest = sb("rest", [P, 2, CH])
    lg = sb("lg", [P, TC, E0])
    ge = sb("ge", [P, TC, E0])
    wts = sb("wts", [P, TC, E0])
    mx = sb("mx", [P, 4, TC])
    wT = sb("wT", [E0, CH])
    mix = sb("mix", [P, TC, D])
    chain = sem("dve_chain")
    var_ready, rstd_ready, xn_ready = sem("var_ready"), sem("rstd_ready"), sem("xn_ready")
    pe_done = sem("pe_done")
    act_done = sem("act_done")
    rest_ready, parts_ready = sem("rest_ready"), sem("parts_ready")
    stored = [sem("stored0"), sem("stored1")]
    lg_taken, lg_ready, wts_ready = sem("lg_taken"), sem("lg_ready"), sem("wts_ready")
    base_ready, mixed = sem("base_ready"), sem("mixed")
    PE_T, PE_Q, PE_K, PE_V, PE_LG, PE_M0, PE_WT, PE_WB, PE_M1, NPE = range(10)
    A_XT, A_QH, A_KH, A_V, A_EXP, A_WT, NA = range(7)
    n_pe = lambda ch, k: ch * NPE + (k + 1)
    n_act = lambda ch, k: ch * NA + (k + 1) + 1
    bT, bQ, bK, bV = 0, 1, 2, 3

    with ph, nc.Block() as block:
        @block.vector
        def _(dve):
            with dve.Fori(0, NCH // 2) as i:
                for s in range(2):
                    ch = 2 * i + s
                    t0 = TB * i + TC * s
                    links = [0]

                    def link(ins):
                        links[0] += 1
                        ins.then_inc(chain, 1)
                        dve.wait_ge(chain, per * ch + links[0])

                    per = 11
                    fixed(dve)
                    for j in range(TC):
                        ins = dve.bn_stats(stats[:, s, j, :], c.x_all[:, bass.ds(t0 + j, 1), :])
                    link(ins)
                    fixed(dve)
                    for j in range(TC):
                        ins = dve.bn_aggr(mv[:, s, j, :], stats[:, s, j, :])
                    link(ins)
                    dve.tensor_scalar(var_eps[:, s, :], mv[:, s, :, 1], 1e-5, None, ALU.add).then_inc(var_ready, 1)
                    dve.wait_ge(rstd_ready, ch + 1)
                    for j in range(TC):
                        ins = dve.tensor_scalar(xn[:, s, j, :], c.x_all[:, bass.ds(t0 + j, 1), :], mv[:, s, j, 0:1],
                                                rstd[:, s, j:j + 1], ALU.subtract, ALU.mult)
                    ins.then_inc(xn_ready, 1)
                    for n, (a, bank) in enumerate(((A_QH, bQ), (A_KH, bK))):
                        dve.wait_ge(act_done, n_act(ch, a))
                        dve.wait_ge(parts_ready, 1 + 2 * ch + n)
                        dve.tensor_tensor(rest[:, n, :], c.ps[:, bank, :], parts[:, s, n, 0, :],
                                          ALU.subtract).then_inc(rest_ready, 1)
                    dve.wait_ge(pe_done, n_pe(ch, PE_LG))
                    gb = tab(c, "gate_b").unsqueeze(1).to_broadcast([P, TC, E0])
                    link(dve.tensor_tensor(lg[:, :, :], c.ps[:, bV, 0:TC * E0].rearrange("p (t e) -> p t e", e=E0), gb, ALU.add))
                    dve.tensor_reduce(mx[:, 0, :], lg[:, :, :], AX_X, ALU.max).then_inc(lg_taken, 1)
                    dve.wait_ge(lg_taken, ch + 1)
                    bc = lambda k: mx[:, k, :].unsqueeze(2).to_broadcast([P, TC, E0])
                    dve.tensor_tensor(lg[:, :, :], lg[:, :, :], bc(0), ALU.subtract).then_inc(lg_ready, 1)
                    dve.wait_ge(act_done, n_act(ch, A_EXP))
                    link(dve.tensor_reduce(mx[:, 1, :], ge[:, :, :], AX_X, ALU.add))
                    link(dve.reciprocal(mx[:, 2, :], mx[:, 1, :]))
                    link(dve.tensor_tensor(ge[:, :, :], ge[:, :, :], bc(2), ALU.mult))
                    link(dve.scalar_tensor_tensor(out=lg[:, :, :], in0=ge[:, :, :], scalar=0.1, in1=ge[:, :, :],
                                                  op0=ALU.is_ge, op1=ALU.mult))
                    link(dve.tensor_reduce(mx[:, 3, :], lg[:, :, :], AX_X, ALU.add))
                    link(dve.scalar_tensor_tensor(out=mx[:, 1, :], in0=mx[:, 3, :], scalar=0.0, in1=mx[:, 3, :],
                                                  op0=ALU.is_equal, op1=ALU.add))
                    link(dve.reciprocal(mx[:, 2, :], mx[:, 1, :]))
                    dve.tensor_tensor(wts[:, :, :], lg[:, :, :], bc(2), ALU.mult).then_inc(wts_ready, 1)
                    dve.wait_ge(pe_done, n_pe(ch, PE_WB))
                    dve.wait_ge(base_ready, ch + 1)
                    link(dve.tensor_tensor(mix[:, :, :], c.ps[:, bV, :].rearrange("p (t d) -> p t d", d=D),
                                           c.acc_all[:, bass.ds(t0, TC), :], ALU.add))
                    for half in range(2):
                        dve.wait_ge(pe_done, n_pe(ch, PE_M1 if half else PE_M0))
                        for e in range(E0):
                            for j in (2 * half, 2 * half + 1):
                                bank = 4 + 2 * (j % 2) + e // 4
                                last = e == E0 - 1
                                out = c.acc_all[:, bass.ds(t0 + j, 1), :] if last else mix[:, j:j + 1, :]
                                src = c.ps[:, bank, (e % 4) * D:(e % 4 + 1) * D].unsqueeze(1)
                                ins = dve.scalar_tensor_tensor(out=out, in0=src, scalar=wts[:, j, e:e + 1], in1=mix[:, j:j + 1, :],
                                                               op0=ALU.mult, op1=ALU.add)
                                ins.then_inc(mixed, 1)
                            dve.wait_ge(mixed, 1 + 32 * ch + 16 * half + 2 * e + 2)
                    assert links[0] == per, links

        @block.gpsimd
        def _(pool):
            for ahead in (act_done, parts_ready, rest_ready, mixed):
                pool.sem_inc(ahead, 1)
            for ahead in stored:
                pool.sem_inc(ahead, 16)
            with pool.Fori(0, NCH // 2) as i:
                for s in range(2):
                    ch = 2 * i + s
                    t0 = TB * i + TC * s
                    pool.wait_ge(var_ready, ch + 1)
                    pool.tensor_tensor(rstd[:, s, :], var_eps[:, s, :], c.neghalf[:, 0:TC], ALU.pow).then_inc(rstd_ready, 1)
                    bo = tab(c, "bo").unsqueeze(1).to_broadcast([P, TC, D])
                    pool.tensor_tensor(c.acc_all[:, bass.ds(t0, TC), :], c.x_all[:, bass.ds(t0, TC), :], bo,
                                       ALU.add).then_inc(base_ready, 1)
                    for n in range(2):
                        pool.wait_ge(rest_ready, 1 + 2 * ch + n + 1)
                        fixed(pool)
                        pool.tensor_copy(parts[:, s, n, 1, :], rest[:, n, :]).then_inc(c.pool_chain, 1)
                        pool.wait_ge(c.pool_chain, 2 * ch + n + 1)
                        pool.tensor_tensor(parts[:, s, n, 2, :], rest[:, n, :], parts[:, s, n, 1, :],
                                           ALU.subtract).then_inc(parts_ready, 1)

        @block.scalar
        def _(act):
            with act.Fori(0, NCH // 2) as i:
                for s in range(2):
                    ch = 2 * i + s
                    act.wait_ge(pe_done, n_pe(ch, PE_T))
                    act.activation(xnT[:, s, :], c.ps[:, bT, :], ACT.Copy).then_inc(act_done, 1)
                    for n, (k, bank) in enumerate(((PE_Q, bQ), (PE_K, bK))):
                        act.wait_ge(pe_done, n_pe(ch, k))
                        act.wait_ge(stored[s], 16 + 32 * i + 16 * n)
                        act.activation(parts[:, s, n, 0, :], c.ps[:, bank, :], ACT.Copy).then_inc(act_done, 1)
                    act.wait_ge(pe_done, n_pe(ch, PE_V))
                    dst = c.v_all[:, bass.ds(NG * i, NG), TC * s:TC * s + TC, :].rearrange("p g t d -> p t g d")
                    act.activation(dst, c.ps[:, bV, :].rearrange("p (t g d) -> p t g d", g=NG, d=G * DH),
                                   ACT.Copy).then_inc(act_done, 1)
                    act.wait_ge(lg_ready, ch + 1)
                    act.activation(ge[:, :, :], lg[:, :, :], ACT.Exp).then_inc(act_done, 1)
                    act.wait_ge(pe_done, n_pe(ch, PE_WT))
                    act.activation(wT[:, :], c.ps[0:E0, bT, :], ACT.Copy).then_inc(act_done, 1)

        @block.sync
        def _(sp):
            with sp.Fori(0, NCH // 2) as i:
                for s in range(2):
                    ch = 2 * i + s
                    for n, dst in enumerate((c.scr_q[0], c.scr_k[0])):
                        sp.wait_ge(parts_ready, 1 + 2 * ch + n + 1)
                        fixed(sp)
                        sp.dma_start(dst[:, :, bass.ds(ch * CH, CH)], parts[:, s, n, :, :]).then_inc(stored[s], 16)
            for s in range(2):
                sp.wait_ge(stored[s], 16 + 32 * (NCH // 2))

        @block.tensor
        def _(pe):
            with pe.Fori(0, NCH // 2) as i:
                for s in range(2):
                    ch = 2 * i + s
                    pe.wait_ge(xn_ready, ch + 1)
                    pe.wait_ge(act_done, 1 + ch * NA)
                    for j in range(TC):
                        ins = pe.transpose(c.ps[:, bT, j * P:(j + 1) * P], xn[:, s, j, :], tab(c, "ident"))
                    ins.then_inc(pe_done, 1)
                    pe.wait_ge(act_done, n_act(ch, A_XT))
                    pe.wait_ge(rest_ready, 1 + 2 * ch)
                    pe.matmul(c.ps[:, bQ, :], w_of(c, "a0_q"), xnT[:, s, :], start=True, stop=True).then_inc(pe_done, 1)
                    pe.matmul(c.ps[:, bK, :], w_of(c, "a0_k"), xnT[:, s, :], start=True, stop=True).then_inc(pe_done, 1)
                    pe.wait_ge(mixed, 1 + 32 * ch)
                    for j in range(TC):
                        ins = pe.matmul(c.ps[:, bV, j * D:(j + 1) * D], xnT[:, s, j * P:(j + 1) * P], w_of(c, "a0_v"),
                                        start=True, stop=True)
                    ins.then_inc(pe_done, 1)
                    pe.wait_ge(act_done, n_act(ch, A_V))
                    for j in range(TC):
                        ins = pe.matmul(c.ps[:, bV, j * E0:(j + 1) * E0], xnT[:, s, j * P:(j + 1) * P], w_of(c, "f0_gate"),
                                        start=True, stop=True)
                    ins.then_inc(pe_done, 1)

                    def experts(js):
                        for j in js:
                            for h in range(2):
                                ins = pe.matmul(c.ps[:, 4 + 2 * (j % 2) + h, :], xnT[:, s, j * P:(j + 1) * P],
                                                w_of(c, "f0_e")[:, h * 4 * D:(h + 1) * 4 * D], start=True, stop=True)
                        ins.then_inc(pe_done, 1)

                    experts((0, 1))
                    pe.wait_ge(wts_ready, ch + 1)
                    for j in range(TC):
                        ins = pe.transpose(c.ps[0:E0, bT, j * P:(j + 1) * P], wts[:, j, :], tab(c, "ident"))
                    ins.then_inc(pe_done, 1)
                    pe.wait_ge(act_done, n_act(ch, A_WT))
                    pe.wait_ge(lg_taken, ch + 1)
                    for j in range(TC):
                        ins = pe.matmul(c.ps[:, bV, j * D:(j + 1) * D], wT[:, j * P:(j + 1) * P], tab(c, "f0_b")[0:E0, :],
                                        start=True, stop=True)
                    ins.then_inc(pe_done, 1)
                    pe.wait_ge(mixed, 1 + 32 * ch + 16)
                    experts((2, 3))



def fixed(eng):
    eng.sem_inc(Ctx.passed, 1)


def stage_attention(nc, c, name, scr_q, scr_k, v_all, out_all):
    ph = ExitStack()
    sb = lambda nm, shape, dt=F32: ph.enter_context(nc.sbuf_tensor(name + nm, shape, dt))
    sem = lambda nm: nc.alloc_semaphore(name + nm)
    qe = sb("qe", [P, 2, 2 * T], BF16)
    ke = sb("ke", [P, 2, 2 * T], BF16)
    prob = sb("prob", [P, 4, G, CH])
    mx = sb("mx", [P, 2, 2, 2, TB + 4])
    mb = sb("mb", [P, 2, 2, 2, 2, TB], BF16)
    mT = sb("mT", [2 * 2 * 2 * TB, 2, P], BF16)
    oT = sb("oT", [P, T])
    rec = sb("rec", [P, TB, G])
    m_loaded = [sem("m_loaded0"), sem("m_loaded1")]
    e_copied = [sem("e_copied0"), sem("e_copied1")]
    e_rows = [sem("e_rows0"), sem("e_rows1")]
    s_filled, s_taken = sem("s_filled"), sem("s_taken")
    x_filled, x_taken = sem("x_filled"), sem("x_taken")
    masked = sem("masked")
    v_staged, v_cleared = sem("v_staged"), sem("v_cleared")
    pv_done = sem("pv_done")
    o_read = sem("o_read")
    max_link, m_split = sem("max_link"), sem("m_split")
    XB, OB = 4, 6

    def rows_of(scr, t, pair, b, g):
        return scr[bass.ds(32 * g + 16 * pair, 16), t:t + 1, bass.ds(T * b, T)].rearrange("p o n -> p (o n)")

    with ph, nc.Block() as block:
        @block.sync
        def _(sp):
            def load(b, g, slot):
                for dst, scr, which in ((c.qm, scr_q, QT), (c.km, scr_k, KT)):
                    for t in range(TERMS):
                        for pair in range(2):
                            sp.dma_start(dst[t:t + 8 * 15 + 1:8, slot, T * pair:T * (pair + 1)],
                                         rows_of(scr, which[t], pair, b, g)).then_inc(m_loaded[slot], 16)

            def copies(n, i, slot):
                sp.wait_ge(m_loaded[slot], 16 * 4 * TERMS * (i + 1))
                fixed(sp)
                sp.wait_ge(pv_done, 1 + NE * n)
                sp.dma_start(qe[:, slot, :], c.qm[:, slot, :]).then_inc(e_copied[slot], 16)
                sp.dma_start(ke[:, slot, :], c.km[:, slot, :]).then_inc(e_copied[slot], 16)

            def max_rows(n, i, slot, turned):
                sp.wait_ge(e_copied[slot], 32 * (i + 1))
                sp.wait_ge(s_taken, 2 + turned)
                for t in range(2):
                    for a in range(2):
                        r = ROWS * a + 8 * t + TERMS
                        k = 2 * TB * (2 * t + a)
                        sp.dma_start(qe[r:r + 1, slot, :].rearrange("o (c n) -> o c n", n=P),
                                     mT[k:k + 2 * TB, slot, :]).then_inc(e_rows[slot], 16)

            load(0, 0, 0)
            load(0, 1, 1)

            def batch(b, first, last):
                for g in range(NG):
                    n, i, s = NG * b + g, 2 * b + g // 2, g % 2
                    turned = NM + 1 if first and g == 0 else USES * n + NM
                    copies(n, i, s)
                    max_rows(n, i, s, turned)
                    if g < 2 or not last:
                        sp.wait_ge(s_filled, turned)
                        fixed(sp)
                        load(b + g // 2, (g + 2) % NG, s)

            batch(0, True, False)
            with sp.Fori(1, B - 1) as b:
                batch(b, False, False)
            batch(B - 1, False, True)
            for s in range(2):
                sp.wait_ge(e_rows[s], 16 * 4 * (N // 2))

        @block.gpsimd
        def _(pool):
            pool.sem_inc(s_taken, 2)
            pool.sem_inc(x_taken, 2)
            pool.sem_inc(pv_done, NE + 1)

            def stage_values(n, s):
                pool.wait_ge(pv_done, 1 + NE * n)
                fixed(pool)
                pool.tensor_copy(c.vst[:, s, :, 0:DH].rearrange("p (t h) d -> p t h d", h=G),
                                 v_all[:, bass.ds(n, 1), :, :].rearrange("p o t (h d) -> p (o t) h d", d=DH)).then_inc(v_staged, 1)

            def masks(n, ks):
                for k in ks:
                    pool.wait_ge(x_taken, 2 + 4 * NE * n + 4 * (k + 1))
                    fixed(pool)
                    blk = prob[:, k % 4, :, 0:P]
                    pool.affine_select(out=blk, in_=blk, compare_op=ALU.is_ge, fill=0.0, base=0,
                                       pattern=[[0, G], [1, P]], channel_multiplier=-1).then_inc(masked, 1)

            def group(n, s, last):
                masks(n, DIAG[:4])
                if not last:
                    stage_values(n + 1, 1 - s)
                masks(n, DIAG[4:])

            pool.memset(c.vst[:, :, :, :], 0.0).then_inc(v_cleared, 1)
            pool.wait_ge(v_cleared, 1)
            pool.memset(c.vst[:, :, :, DH:DH + 1], 1.0).then_inc(v_cleared, 1)
            pool.wait_ge(v_cleared, 2)
            stage_values(0, 0)
            with pool.Fori(0, N // 2 - 1) as i:
                for s in range(2):
                    group(2 * i + s, s, False)
            group(N - 2, 0, False)
            group(N - 1, 1, True)

        @block.scalar
        def _(act):
            def step(n, k, hh):
                w = EXP_STEPS[k][2]
                if hh == 0:
                    act.wait_ge(pv_done, 1 + NE * n + NE + k - 3)
                act.wait_ge(x_filled, 4 * NE * n + 4 * k + hh + 1)
                act.activation(prob[:, k % 4, hh, 0:w], c.ps[:, XB + hh % 2, 0:w], ACT.Exp, scale=DH ** -0.5).then_inc(x_taken, 1)

            def read_out(n):
                act.wait_ge(pv_done, 1 + NE * (n + 2))
                act.activation(oT[:, :].rearrange("p (b n) -> p b n", b=2), c.ps[:, OB:OB + 2, :], ACT.Copy).then_inc(o_read, 1)

            def group(n, before):
                for k in range(NE):
                    for hh in range(G):
                        step(n, k, hh)
                        if (k, hh) == (1, 1) and before:
                            read_out(n - 1)

            group(0, False)
            group(1, True)
            with act.Fori(1, N // 2) as i:
                for s in range(2):
                    group(2 * i + s, True)
            read_out(N - 1)

        @block.vector
        def _(dve):
            def maximum(n, s, k, use, bank):
                if k < NM:
                    pair, (qi, k0, w, cl, _) = k // (NM // 2), MAX_PIECES[k % (NM // 2)]
                    dve.wait_ge(s_filled, use + 1)
                    dve.tensor_reduce(mx[:, s, :, pair, cl], c.ps[:, bank:bank + 2, 0:w], AX_X, ALU.max).then_inc(s_taken, 1)
                    return
                dve.wait_ge(s_taken, 2 + use)
                flat = lambda a, b: mx[:, s, :, :, a:b]
                dve.tensor_tensor(flat(4, TB), flat(4, TB), flat(TB, TB + 4), ALU.max).then_inc(max_link, 1)
                dve.wait_ge(max_link, 2 * n + 1)
                dve.tensor_copy(mb[:, s, 0, :, :, :], flat(0, TB)).then_inc(max_link, 1)
                dve.wait_ge(max_link, 2 * n + 2)
                dve.tensor_tensor(mb[:, s, 1, :, :, :], flat(0, TB), mb[:, s, 0, :, :, :], ALU.subtract).then_inc(m_split, 1)
                dve.wait_ge(s_filled, use + 1)
                dve.tensor_copy(mT[:, s, :], c.ps[0:4 * 2 * TB, bank, 0:P // 2].bitcast(BF16)).then_inc(s_taken, 1)

            def normalise(n, use, bank):
                dve.wait_ge(s_filled, use + 1)
                o = c.ps[:, bank:bank + 2, :].rearrange("p b (t h r) -> p (b t) h r", h=G, r=32)
                dve.reciprocal(rec[:, :, :], o[:, :, :, DH]).then_inc(c.norm_link, 1)
                dve.wait_ge(c.norm_link, c.norms + n + 1)
                dve.tensor_tensor(out_all[:, bass.ds(n, 1), :, :].rearrange("p o t (h d) -> p (o t) h d", d=DH), o[:, :, :, 0:DH],
                                  rec[:, :, :].unsqueeze(3).to_broadcast([P, TB, G, DH]), ALU.mult).then_inc(s_taken, 1)

            def ring(uses):
                for what, n, _, s, k, use, bank, _ in uses:
                    if what == "turn":
                        normalise(n, use, bank)
                    else:
                        maximum(n, s, k, use, bank)

            ring(first_uses())
            ring(ring_uses(0, 0, 0, first=True))
            ring(ring_uses(1, 0, 1))
            with dve.Fori(1, N // 2 - 1) as i:
                for s in range(2):
                    ring(ring_uses(2 * i + s, i, s))
            ring(ring_uses(N - 2, N // 2 - 1, 0, follow=1))
            ring(ring_uses(N - 1, N // 2 - 1, 1, follow=0))
            dve.wait_ge(s_taken, 2 + last_turn()[5])
            ring([last_turn()])

        @block.tensor
        def _(pe):
            def ring_use(what, n, i, s, k, use, bank, _):
                pe.wait_ge(s_taken, use + 1)
                if what == "turn":
                    pe.wait_ge(o_read, n + 1)
                    for t in range(TB):
                        ins = pe.transpose(c.ps[:, bank + t // 4, P * (t % 4):P * (t % 4 + 1)], oT[:, P * t:P * (t + 1)], tab(c, "ident"))
                    ins.then_inc(s_filled, 1)
                    return
                if k == NM:
                    pe.wait_ge(m_split, n + 1)
                    fixed(pe)
                    pe.transpose(c.ps[0:4 * 2 * TB, bank, 0:P // 2].bitcast(BF16),
                                 mb[:, s, :, :, :, :].rearrange("p t a c q -> p (t a c q)"), c.ident_bf[:, :]).then_inc(s_filled, 1)
                    return
                if k == 0:
                    pe.wait_ge(m_loaded[s], 16 * 4 * TERMS * (i + 1))
                pair, (qi, k0, w, _, diag) = k // (NM // 2), MAX_PIECES[k % (NM // 2)]
                for a in range(2):
                    rows = slice(ROWS * a, ROWS * (a + 1))
                    at = T * pair
                    ins = pe.matmul(c.ps[:, bank + a, 0:w], c.qm[rows, s, at + P * qi:at + P * (qi + 1)],
                                    c.km[rows, s, at + k0:at + k0 + w], start=True, stop=not diag)
                if diag:
                    for a in range(2):
                        ins = pe.matmul(c.ps[:, bank + a, w - P:w], c.ident_bf[:, :], c.mask_bf[:, :], start=False, stop=True)
                ins.then_inc(s_filled, 1)

            def scores(n, i, s, k, hh):
                j, q0, w = EXP_STEPS[k]
                if k == 0 and hh == 0:
                    pe.wait_ge(e_rows[s], 16 * 4 * (i + 1))
                pair, a = hh // 2, hh % 2
                rows = slice(ROWS * a, ROWS * (a + 1))
                at = T * pair
                pe.wait_ge(x_taken, 4 * NE * n + 4 * k + hh + 1)
                pe.matmul(c.ps[:, XB + a, 0:w], ke[rows, s, at + P * j:at + P * (j + 1)], qe[rows, s, at + q0:at + q0 + w],
                          start=True, stop=True).then_inc(x_filled, 1)

            def values(n, s, k):
                j, q0, w = EXP_STEPS[k]
                if k == 0:
                    pe.wait_ge(v_staged, n + 1)
                if k in DIAG:
                    pe.wait_ge(masked, len(DIAG) * n + DIAG.index(k) + 1)
                else:
                    pe.wait_ge(x_taken, 2 + 4 * NE * n + 4 * (k + 1))
                half = q0 // CH
                for hh in range(G):
                    ins = pe.matmul(c.ps[32 * hh:32 * hh + 32, OB + half, q0 - CH * half:q0 - CH * half + w],
                                    c.vst[:, s, G * j + hh, :], prob[:, k % 4, hh, 0:w],
                                    start=(j == 0), stop=(j == 4 * half + 3))
                ins.then_inc(pv_done, 1)

            def group(n, i, s, first=False, follow=2):
                todo = ring_uses(n, i, s, first, follow)
                for k in range(NE):
                    mine = [u for u in todo if u[-1] == k]
                    scores(n, i, s, k, 0)
                    for u in mine[:1]:
                        ring_use(*u)
                    scores(n, i, s, k, 1)
                    if k >= 2:
                        if k == 2 and not first:
                            pe.wait_ge(o_read, n)
                        values(n, s, k - 2)
                    elif not first:
                        values(n - 1, 1 - s, NE - 2 + k)
                    scores(n, i, s, k, 2)
                    for u in mine[1:2]:
                        ring_use(*u)
                    scores(n, i, s, k, 3)
                    for u in mine[2:]:
                        ring_use(*u)

            for u in first_uses():
                ring_use(*u)
            group(0, 0, 0, first=True)
            group(1, 0, 1)
            with pe.Fori(1, N // 2 - 1) as i:
                for s in range(2):
                    group(2 * i + s, i, s)
            group(N - 2, N // 2 - 1, 0, follow=1)
            group(N - 1, N // 2 - 1, 1, follow=0)
            for k in (NE - 2, NE - 1):
                values(N - 1, 1, k)
            ring_use(*last_turn())
    c.norms += N



def by_group(ap4, t, n):
    return ap4[:, :, t:t + n, :].rearrange("p g t d -> p t g d")


def stage_between(nc, c):
    ph = ExitStack()
    sb = lambda name, shape, dt=F32: ph.enter_context(nc.sbuf_tensor("p3_" + name, shape, dt))
    sem = lambda name: nc.alloc_semaphore("p3_" + name)
    aos, aoT = sb("aos", [P, TC, D]), sb("aoT", [P, CH])
    stats, mv = sb("stats", [P, TC, 6]), sb("mv", [P, TC, 2])
    var_eps, rstd = sb("var_eps", [P, TC]), sb("rstd", [P, TC])
    ms, r1 = sb("ms", [P, TC]), sb("r1", [P, 2, TC])
    xn, xnT, hT = sb("xn", [P, TC, D]), sb("xnT", [P, 2, CH]), sb("hT", [P, 2, CH])
    rqk = sb("rqk", [P, 2, CH])
    qhead = sb("qhead", [P, 2 * G, CH])
    ktok, vtok = sb("ktok", [P, TC, D]), sb("vtok", [P, TC, D])
    vhead = c.vst[:, :, :, :].rearrange("p s n r -> p (s n r)").rearrange("p (u r) -> p u r", u=TC * NG)
    sc = sb("sc", [P, 4, G * P])
    qk, sq = sb("qk", [P, TC, 2 * D]), sb("sq", [P, TC, 2 * D])
    hs, hr = sb("hs", [P, TC * 2 * H]), sb("hr", [P, TC * 2 * H])
    state, step = sb("state", [P, 2, TC, D]), sb("step", [P, TC, D])
    sqx = sb("sqx", [P, TC, D])
    parts = sb("parts", [P, 2, 3, CH], BF16)
    rest = sb("rest", [P, 2, CH])
    chain_a, chain_b, hs_chain, pool_chain, cleared = (sem(n) for n in ("chain_a", "chain_b", "hs_chain", "pool_chain", "cleared"))
    EVENTS = {
        "pe_a": ["T_AO", "WO", "T_XN"], "act_a": ["AOT", "XNT", "XN1"], "dve_a": ["X1", "VAR", "XN", "MS"],
        "pool_a": ["AO", "RSTD", "R1", "HT"],
        "pe_b": ["RQ", "RK", "KV", "F0", "F1", "F2", "F3", "U", "TQ", "TK"],
        "act_b": ["QHEAD", "V", "F0", "F1", "F2", "F3", "SQRT", "FQH", "FKH", "Y"],
        "dve_b": ["RQ", "RK", "KTOK", "STATE", "HS", "QK", "FQR", "FKR", "YSTAT"],
        "pool_b": ["SQ", "FQL", "FKL"]}
    done = {name: sem(name) for name in EVENTS}
    scored, masked, valued = sem("scored"), sem("masked"), sem("valued")
    stored = [sem("stored0"), sem("stored1")]
    NR = TC * NG

    def at(who, ch, what):
        return 1 + len(EVENTS[who]) * ch + EVENTS[who].index(what) + 1

    def before(who, ch):
        return 1 + len(EVENTS[who]) * ch

    def chunks(eng, ahead, behind):
        ahead(0, 0)
        with eng.Fori(0, NCH // 2 - 1) as i:
            behind(i, 0, (i, 1))
            behind(i, 1, (i + 1, 0))
        behind(NCH // 2 - 1, 0, (NCH // 2 - 1, 1))
        behind(NCH // 2 - 1, 1, None)

    with ph, nc.Block() as block:
        @block.gpsimd
        def _(pool):
            for name in EVENTS:
                pool.sem_inc(done[name], 1)
            pool.sem_inc(masked, 2)
            pool.sem_inc(valued, 4)
            for ahead in stored:
                pool.sem_inc(ahead, 16)
            pool.memset(vhead[:, :, :], 0.0).then_inc(cleared, 1)

            def low_parts(ch, n, src):
                pool.wait_ge(done["dve_b"], at("dve_b", ch, src))
                fixed(pool)
                pool.tensor_copy(parts[:, n, 1, :], rest[:, n, :]).then_inc(pool_chain, 1)
                pool.wait_ge(pool_chain, 2 * ch + n + 1)
                pool.tensor_tensor(parts[:, n, 2, :], rest[:, n, :], parts[:, n, 1, :], ALU.subtract).then_inc(done["pool_b"], 1)

            def gather(i, s):
                ch = 2 * i + s
                pool.wait_ge(done["pe_a"], before("pe_a", ch))
                fixed(pool)
                pool.tensor_copy(aos[:, :, :].rearrange("p t (g d) -> p t g d", g=NG),
                                 by_group(c.ao_all[:, bass.ds(NG * i, NG), :, :], TC * s, TC)).then_inc(done["pool_a"], 1)

            def powers(i, s):
                ch = 2 * i + s
                pool.wait_ge(done["dve_a"], at("dve_a", ch, "VAR"))
                pool.tensor_tensor(rstd[:, :], var_eps[:, :], c.neghalf[:, 0:TC], ALU.pow).then_inc(done["pool_a"], 1)
                pool.wait_ge(done["dve_a"], at("dve_a", ch, "MS"))
                pool.tensor_tensor(r1[:, s, :], ms[:, :], c.neghalf[:, 0:TC], ALU.pow).then_inc(done["pool_a"], 1)

            def weighted(i, s):
                ch = 2 * i + s
                pool.wait_ge(done["act_a"], at("act_a", ch, "XNT"))
                fixed(pool)
                pool.tensor_scalar(hT[:, s, :], xnT[:, s, :], col(c, "n1_w"), None, ALU.mult).then_inc(done["pool_a"], 1)

            def ahead_all(i, s):
                gather(i, s)
                powers(i, s)
                weighted(i, s)

            def behind(i, s, nxt):
                ch = 2 * i + s
                if nxt:
                    gather(*nxt)
                pool.wait_ge(done["act_b"], at("act_b", ch, "F3"))
                pool.tensor_tensor(sq[:, :, :], qk[:, :, :], qk[:, :, :], ALU.mult).then_inc(done["pool_b"], 1)
                if nxt:
                    powers(*nxt)
                low_parts(ch, 0, "FQR")
                low_parts(ch, 1, "FKR")
                if nxt:
                    weighted(*nxt)

            chunks(pool, ahead_all, behind)

        @block.scalar
        def _(act):
            def high_part(ch, n, what):
                act.wait_ge(done["pe_b"], at("pe_b", ch, what))
                act.wait_ge(stored[n], 16 * (1 + ch))
                act.activation(parts[:, n, 0, :], c.ps[:, 2 + n, :], ACT.Copy, scale=col(c, ("qn_w", "kn_w")[n])).then_inc(done["act_b"], 1)

            def turned_outputs(i, s):
                act.wait_ge(done["pe_a"], at("pe_a", 2 * i + s, "T_AO"))
                act.activation(aoT[:, :], c.ps[:, 0, :], ACT.Copy).then_inc(done["act_a"], 1)

            def normed(i, s):
                ch, t0 = 2 * i + s, TB * i + TC * s
                act.wait_ge(done["pe_a"], at("pe_a", ch, "T_XN"))
                act.activation(xnT[:, s, :], c.ps[:, 0, :], ACT.Copy).then_inc(done["act_a"], 1)
                act.activation(c.xn1_all[:, bass.ds(t0, TC), :], xn[:, :, :], ACT.Copy).then_inc(done["act_a"], 1)

            def ahead_all(i, s):
                turned_outputs(i, s)
                normed(i, s)

            def behind(i, s, nxt):
                ch = 2 * i + s
                act.wait_ge(valued, 4 + NR * ch)
                act.wait_ge(done["dve_b"], at("dve_b", ch, "RQ"))
                for hh in range(2 * G):
                    ins = act.activation(qhead[:, hh, :], rqk[:, 0, :], ACT.Copy, scale=c.head_cols[:, hh:hh + 1])
                ins.then_inc(done["act_b"], 1)
                act.wait_ge(done["pe_b"], at("pe_b", ch, "KV"))
                kv = c.ps[:, 4:6, :].rearrange("p b (t x d) -> p (b t) x d", x=2, d=D)
                for hh in range(G):
                    a = (4 * DH + DH) * hh
                    act.activation(vhead[:, :, a:a + DH].rearrange("p (t g) d -> p t g d", g=NG),
                                   kv[:, :, 1, :].rearrange("p t (g r) -> p t g r", g=NG)[:, :, :, DH * hh:DH * (hh + 1)], ACT.Copy)
                act.activation(vtok[:, :, :], kv[:, :, 1, :], ACT.Copy).then_inc(done["act_b"], 1)
                act.wait_ge(done["pool_a"], at("pool_a", ch, "R1"))
                for j in range(TC):
                    act.wait_ge(done["pe_b"], at("pe_b", ch, f"F{j}"))
                    act.activation(qk[:, j, :], c.ps[:, 2 + j, 0:2 * D], ACT.Copy, scale=r1[:, s, j:j + 1])
                    t = TC * s + j
                    act.activation(c.v_all[:, bass.ds(NG * i, NG), t:t + 1, :].rearrange("p g o d -> p (g o) d"),
                                   c.ps[:, 2 + j, 2 * D:3 * D].rearrange("p (g d) -> p g d", g=NG), ACT.Copy,
                                   scale=r1[:, s, j:j + 1]).then_inc(done["act_b"], 1)
                if nxt:
                    turned_outputs(*nxt)
                act.wait_ge(done["dve_b"], at("dve_b", ch, "HS"))
                act.activation(hr[:, :], hs[:, :], ACT.Sqrt).then_inc(done["act_b"], 1)
                high_part(ch, 0, "TQ")
                high_part(ch, 1, "TK")
                act.wait_ge(valued, 4 + NR * (ch + 1))
                act.activation(c.yT_all[:, bass.ds(CH * ch, CH)], c.ps[:, 6, :], ACT.Copy).then_inc(done["act_b"], 1)
                if nxt:
                    normed(*nxt)

            act.wait_ge(cleared, 2)
            chunks(act, ahead_all, behind)

        @block.vector
        def _(dve):
            def residual(i, s):
                ch, t0 = 2 * i + s, TB * i + TC * s
                dve.wait_ge(done["pe_a"], at("pe_a", ch, "WO"))
                dve.tensor_tensor(c.x_all[:, bass.ds(t0, TC), :], c.ps[:, 1, :].rearrange("p (t d) -> p t d", d=D),
                                  c.acc_all[:, bass.ds(t0, TC), :], ALU.add).then_inc(done["dve_a"], 1)
                dve.wait_ge(done["dve_a"], at("dve_a", ch, "X1"))
                fixed(dve)
                for j in range(TC):
                    ins = dve.bn_stats(stats[:, j, :], c.x_all[:, bass.ds(t0 + j, 1), :])
                ins.then_inc(chain_a, 1)
                dve.wait_ge(chain_a, 3 * ch + 1)
                fixed(dve)
                for j in range(TC):
                    ins = dve.bn_aggr(mv[:, j, :], stats[:, j, :])
                ins.then_inc(chain_a, 1)
                dve.wait_ge(chain_a, 3 * ch + 2)
                dve.tensor_scalar(var_eps[:, :], mv[:, :, 1], 1e-5, None, ALU.add).then_inc(done["dve_a"], 1)

            def norm(i, s):
                ch, t0 = 2 * i + s, TB * i + TC * s
                dve.wait_ge(done["pool_a"], at("pool_a", ch, "RSTD"))
                dve.wait_ge(done["act_a"], before("act_a", ch))
                for j in range(TC):
                    ins = dve.tensor_scalar(xn[:, j, :], c.x_all[:, bass.ds(t0 + j, 1), :], mv[:, j, 0:1],
                                            rstd[:, j:j + 1], ALU.subtract, ALU.mult)
                ins.then_inc(done["dve_a"], 1)
                dve.wait_ge(done["dve_a"], at("dve_a", ch, "XN"))
                for j in range(TC):
                    ins = dve.tensor_tensor_reduce(out=sqx[:, j, :], in0=xn[:, j, :], in1=xn[:, j, :], scale=1.0, scalar=0.0,
                                                   op0=ALU.mult, op1=ALU.add, accum_out=ms[:, j:j + 1])
                ins.then_inc(chain_a, 1)
                dve.wait_ge(chain_a, 3 * ch + 3)
                dve.tensor_scalar(ms[:, :], ms[:, :], 1.0 / D, 1.1920929e-07, ALU.mult, ALU.add).then_inc(done["dve_a"], 1)

            def ahead_all(i, s):
                residual(i, s)
                norm(i, s)

            def behind(i, s, nxt):
                ch = 2 * i + s

                def mask(tile):
                    for u in range(NG * tile, NG * (tile + 1)):
                        dve.wait_ge(scored, NR * ch + u + 1)
                        dve.wait_ge(valued, NR * ch + u + 1)
                        dve.tensor_tensor(sc[:, u % 4, :].rearrange("p (h n) -> p h n", n=P),
                                          c.ps[:, 4 + u % 2, :].rearrange("p (h n) -> p h n", n=P),
                                          tab(c, "tri").unsqueeze(1).to_broadcast([P, G, P]), ALU.mult).then_inc(masked, 1)

                def left(n, what):
                    dve.wait_ge(done["act_b"], at("act_b", ch, what))
                    dve.wait_ge(done["pool_b"], before("pool_b", ch))
                    dve.scalar_tensor_tensor(out=rest[:, n, :], in0=c.ps[:, 2 + n, :], scalar=col(c, ("qn_w", "kn_w")[n]),
                                             in1=parts[:, n, 0, :], op0=ALU.mult, op1=ALU.subtract).then_inc(done["dve_b"], 1)

                for n, (k, g) in enumerate((("RQ", "gq"), ("RK", "gk"))):
                    dve.wait_ge(done["pe_b"], at("pe_b", ch, k))
                    dve.tensor_tensor(rqk[:, n, :].rearrange("p (t n) -> p t n", n=P),
                                      c.ps[:, 2 + n, :].rearrange("p (t n) -> p t n", n=P),
                                      tab(c, g).unsqueeze(1).to_broadcast([P, TC, P]), ALU.mult).then_inc(done["dve_b"], 1)
                dve.wait_ge(done["act_b"], at("act_b", ch, "V"))
                kv = c.ps[:, 4:6, :].rearrange("p b (t x d) -> p (b t) x d", x=2, d=D)
                dve.tensor_tensor(ktok[:, :, :], kv[:, :, 0, :], tab(c, "gktok").unsqueeze(1).to_broadcast([P, TC, D]),
                                  ALU.mult).then_inc(done["dve_b"], 1)
                dve.wait_ge(done["pe_b"], at("pe_b", ch, "U"))
                dve.tensor_tensor(step[:, :, :], c.ps[:, 7, :].rearrange("p (t d) -> p t d", d=D),
                                  tab(c, "carry").unsqueeze(1).to_broadcast([P, TC, D]), ALU.mult).then_inc(chain_b, 1)
                for j in range(TC):
                    dve.wait_ge(chain_b, 5 * ch + j + 1)
                    dst = state[:, s, j + 1, :] if j + 1 < TC else state[:, 1 - s, 0, :]
                    if s == 1 and j == TC - 1:
                        fixed(dve)
                        ins = dve.memset(dst, 0.0)
                    else:
                        ins = dve.scalar_tensor_tensor(out=dst, in0=state[:, s, j, :], scalar=col(c, "g128"), in1=step[:, j, :],
                                                       op0=ALU.mult, op1=ALU.add)
                    ins.then_inc(chain_b, 1)
                dve.wait_ge(chain_b, 5 * (ch + 1))
                dve.sem_inc(done["dve_b"], 1)
                mask(0)
                mask(1)
                if nxt:
                    residual(*nxt)
                dve.wait_ge(done["pool_b"], at("pool_b", ch, "SQ"))
                dve.tensor_reduce(hr[:, :], sq[:, :, :].rearrange("p t (h d) -> p (t h) d", d=DH), AX_X,
                                  ALU.add).then_inc(hs_chain, 1)
                dve.wait_ge(hs_chain, 2 * ch + 1)
                dve.tensor_scalar(hr[:, :], hr[:, :], 1.0 / DH, 1.1920929e-07, ALU.mult, ALU.add).then_inc(hs_chain, 1)
                dve.wait_ge(hs_chain, 2 * ch + 2)
                dve.reciprocal(hs[:, :], hr[:, :]).then_inc(done["dve_b"], 1)
                mask(2)
                dve.wait_ge(done["act_b"], at("act_b", ch, "SQRT"))
                heads = qk[:, :, :].rearrange("p t (h d) -> p (t h) d", d=DH)
                dve.tensor_tensor(heads, heads, hr[:, :].unsqueeze(2).to_broadcast([P, TC * 2 * H, DH]),
                                  ALU.mult).then_inc(done["dve_b"], 1)
                if nxt:
                    norm(*nxt)
                mask(3)
                left(0, "FQH")
                left(1, "FKH")
                dve.wait_ge(done["act_b"], at("act_b", ch, "Y"))
                fixed(dve)
                dve.bn_stats(c.gn_stats[:, bass.ds(ch, 1), :].rearrange("p o k -> p (o k)"), c.ps[:, 6, :]).then_inc(done["dve_b"], 1)

            dve.memset(state[:, 0, 0, :], 0.0).then_inc(cleared, 1)
            dve.wait_ge(cleared, 2)
            chunks(dve, ahead_all, behind)

        @block.sync
        def _(sp):
            with sp.Fori(0, NCH) as ch:
                for n, (dst, what) in enumerate(((c.scr_q[1], "FQL"), (c.scr_k[1], "FKL"))):
                    sp.wait_ge(done["pool_b"], at("pool_b", ch, what))
                    fixed(sp)
                    sp.dma_start(dst[:, :, bass.ds(ch * CH, CH)], parts[:, n, :, :]).then_inc(stored[n], 16)
            for k in range(2):
                sp.wait_ge(stored[k], 16 * (1 + NCH))

        @block.tensor
        def _(pe):
            def each(phase, fn):
                for j in range(TC):
                    ins = fn(j)
                ins.then_inc(done[phase], 1)

            tile = lambda j: slice(j * P, (j + 1) * P)
            ident = tab(c, "ident")

            def turn_outputs(i, s):
                ch = 2 * i + s
                pe.wait_ge(done["pool_a"], at("pool_a", ch, "AO"))
                pe.wait_ge(done["act_a"], before("act_a", ch))
                each("pe_a", lambda j: pe.transpose(c.ps[:, 0, tile(j)], aos[:, j, :], ident))

            def project_outputs(i, s):
                ch = 2 * i + s
                pe.wait_ge(done["act_a"], at("act_a", ch, "AOT"))
                pe.wait_ge(done["dve_a"], before("dve_a", ch))
                each("pe_a", lambda j: pe.matmul(c.ps[:, 1, tile(j)], aoT[:, tile(j)], w_of(c, "a0_o"), start=True, stop=True))

            def turn_normed(i, s):
                pe.wait_ge(done["dve_a"], at("dve_a", 2 * i + s, "XN"))
                each("pe_a", lambda j: pe.transpose(c.ps[:, 0, tile(j)], xn[:, j, :], ident))

            def ahead_all(i, s):
                turn_outputs(i, s)
                project_outputs(i, s)
                turn_normed(i, s)

            def behind(i, s, nxt):
                ch = 2 * i + s
                b = done["pe_b"]

                def scores(u):
                    t, g = u // NG, u % NG
                    rows, heads = slice(ROWS * (g // 2), ROWS * (g // 2 + 1)), slice(G * (g % 2), G * (g % 2 + 1))
                    pe.wait_ge(masked, NR * ch + u + 1)
                    pe.matmul(c.ps[:, 4 + u % 2, :].rearrange("p (h n) -> p h n", n=P), rqk[rows, 1, tile(t)], qhead[rows, heads, tile(t)],
                              start=True, stop=True).then_inc(scored, 1)

                def values(u):
                    t, g = u // NG, u % NG
                    if g == 0:
                        pe.matmul(c.ps[:, 6, tile(t)], state[:, s, t, :], rqk[:, 0, tile(t)], start=True, stop=False)
                    pe.wait_ge(masked, 2 + NR * ch + u + 1)
                    for hh in range(G):
                        ins = pe.matmul(c.ps[32 * g:32 * (g + 1), 6, tile(t)], vhead[:, u, 32 * hh:32 * (hh + 1)],
                                        sc[:, u % 4, tile(hh)], start=False, stop=(hh == G - 1))
                    ins.then_inc(valued, 1)

                def ring(t):
                    for u in range(NG * t, NG * (t + 1)):
                        scores(u)
                        if u >= 2:
                            values(u - 2)

                pe.wait_ge(done["act_a"], at("act_a", ch, "XNT"))
                pe.wait_ge(done["dve_b"], before("dve_b", ch))
                pe.wait_ge(done["act_b"], before("act_b", ch))
                pe.matmul(c.ps[:, 2, :], w_of(c, "a1_q"), xnT[:, s, :], start=True, stop=True).then_inc(b, 1)
                pe.matmul(c.ps[:, 3, :], w_of(c, "a1_k"), xnT[:, s, :], start=True, stop=True).then_inc(b, 1)
                each("pe_b", lambda j: pe.matmul(c.ps[:, 4 + j // 2, 2 * D * (j % 2):2 * D * (j % 2 + 1)], xnT[:, s, tile(j)],
                                                 w_of(c, "a1_kv"), start=True, stop=True))
                pe.wait_ge(done["pool_a"], at("pool_a", ch, "HT"))
                for j in range(TC):
                    pe.wait_ge(done["dve_b"], at("dve_b", ch, "RQ" if j == 0 else "RK" if j == 1 else "KTOK"))
                    pe.matmul(c.ps[:, 2 + j, 0:3 * D], hT[:, s, tile(j)], w_of(c, "f1_qkv"), start=True, stop=True).then_inc(b, 1)
                each("pe_b", lambda j: pe.matmul(c.ps[:, 7, tile(j)], ktok[:, j, :], vtok[:, j, :], start=True, stop=True))
                pe.wait_ge(done["dve_b"], at("dve_b", ch, "STATE"))
                pe.wait_ge(done["act_b"], at("act_b", ch, "F3"))
                ring(0)
                if nxt:
                    turn_outputs(*nxt)
                ring(1)
                if nxt:
                    project_outputs(*nxt)
                ring(2)
                ring(3)
                values(NR - 2)
                values(NR - 1)
                pe.wait_ge(done["dve_b"], at("dve_b", ch, "QK"))
                for n in range(2):
                    each("pe_b", lambda j: pe.transpose(c.ps[:, 2 + n, tile(j)], qk[:, j, n * D:(n + 1) * D], ident))
                if nxt:
                    turn_normed(*nxt)

            chunks(pe, ahead_all, behind)


def stage_groupnorm(nc, c):
    ph = ExitStack()
    sb = lambda name, shape, dt=F32: ph.enter_context(nc.sbuf_tensor("g_" + name, shape, dt))
    sem = lambda name: nc.alloc_semaphore("g_" + name)
    mv = sb("mv", [P, B, 2])
    st = sb("st", [P, 6, B])
    summed, chain, squared, var_ready, rstd_ready, scaled = (sem(n) for n in ("summed", "chain", "squared", "var_ready", "rstd_ready", "scaled"))
    DEV, VAR, EPS, RSTD, SCALE, BIAS = range(6)

    with ph, nc.Block() as block:
        @block.tensor
        def _(pe):
            pe.wait_ge(chain, B)
            pe.matmul(c.ps[:, 0, 0:B], tab(c, "head_mean"), mv[:, :, 0], start=True, stop=True).then_inc(summed, 1)
            pe.wait_ge(squared, 1)
            pe.matmul(c.ps[:, 1, 0:B], tab(c, "head_mean"), st[:, VAR, :], start=True, stop=True).then_inc(summed, 1)

        @block.vector
        def _(dve):
            links = [0]

            def link(ins):
                links[0] += 1
                ins.then_inc(chain, 1)
                dve.wait_ge(chain, links[0])

            for b in range(B):
                ins = dve.bn_aggr(mv[:, b, :], c.gn_stats[:, 2 * b:2 * b + 2, :])
                link(ins)
            dve.wait_ge(summed, 1)
            link(dve.tensor_tensor(st[:, DEV, :], mv[:, :, 0], c.ps[:, 0, 0:B], ALU.subtract))
            link(dve.tensor_tensor(st[:, VAR, :], st[:, DEV, :], st[:, DEV, :], ALU.mult))
            dve.tensor_tensor(st[:, VAR, :], st[:, VAR, :], mv[:, :, 1], ALU.add).then_inc(squared, 1)
            dve.wait_ge(summed, 2)
            dve.tensor_scalar(st[:, EPS, :], c.ps[:, 1, 0:B], 1e-5, None, ALU.add).then_inc(var_ready, 1)
            dve.wait_ge(rstd_ready, 1)
            link(dve.tensor_scalar(st[:, SCALE, :], st[:, RSTD, :], col(c, "gn_w"), None, ALU.mult))
            link(dve.tensor_tensor(st[:, BIAS, :], c.ps[:, 0, 0:B], st[:, SCALE, :], ALU.mult))
            dve.tensor_scalar(st[:, BIAS, :], st[:, BIAS, :], -1.0, col(c, "gn_b"), ALU.mult, ALU.add).then_inc(scaled, 1)

        @block.gpsimd
        def _(pool):
            pool.wait_ge(var_ready, 1)
            pool.tensor_tensor(st[:, RSTD, :], st[:, EPS, :], c.neghalf[:, 0:B], ALU.pow).then_inc(rstd_ready, 1)

        @block.scalar
        def _(act):
            act.wait_ge(scaled, 1)
            for b in range(B):
                y = c.yT_all[:, T * b:T * (b + 1)]
                act.activation(y, y, ACT.Identity, scale=st[:, SCALE, b:b + 1], bias=st[:, BIAS, b:b + 1])


def stage_after(nc, c):
    ph = ExitStack()
    sb = lambda name, shape, dt=F32: ph.enter_context(nc.sbuf_tensor("p6_" + name, shape, dt))
    sem = lambda name: nc.alloc_semaphore("p6_" + name)
    aos, aoT = sb("aos", [P, TC, D]), sb("aoT", [P, CH])
    yT = sb("yT", [P, CH])
    x2, x2n = sb("x2", [P, TC, D]), sb("x2n", [P, TC, D])
    base, junk = sb("base", [P, TC, D]), sb("junk", [P, D])
    ms, r2 = sb("ms", [P, TC]), sb("r2", [P, TC])
    xfT = sb("xfT", [P, CH])
    chain = sem("dve_chain")
    PE = ["T_AO", "WO", "RO", "T_XF", "GATE"]
    AC = ["AOT", "YT", "X2N", "XFT", "XFT_ALL"]
    DV = ["X2", "BASE", "MS", "LG"]
    PO = ["AO", "X2", "R2"]
    pe_done, act_done, dve_done, pool_done = sem("pe_done"), sem("act_done"), sem("dve_done"), sem("pool_done")
    n_of = {id(pe_done): PE, id(act_done): AC, id(dve_done): DV, id(pool_done): PO}

    def at(done, ch, what):
        return 1 + len(n_of[id(done)]) * ch + n_of[id(done)].index(what) + 1

    with ph, nc.Block() as block:
        @block.gpsimd
        def _(pool):
            for ahead in (pe_done, act_done, dve_done, pool_done):
                pool.sem_inc(ahead, 1)
            with pool.Fori(0, NCH // 2) as i:
                for s in range(2):
                    ch, t0 = 2 * i + s, TB * i + TC * s
                    pool.wait_ge(pe_done, 1 + len(PE) * ch)
                    fixed(pool)
                    pool.tensor_copy(aos[:, :, :].rearrange("p t (g d) -> p t g d", g=NG),
                                     by_group(c.ao_all[:, bass.ds(NG * i, NG), :, :], TC * s, TC)).then_inc(pool_done, 1)
                    pool.wait_ge(dve_done, 1 + len(DV) * ch)
                    fixed(pool)
                    pool.tensor_copy(x2[:, :, 0:MZ], c.xn1_all[:, bass.ds(t0, TC), 0:MZ]).then_inc(pool_done, 1)
                    pool.wait_ge(dve_done, at(dve_done, ch, "MS"))
                    pool.tensor_tensor(r2[:, :], ms[:, :], c.neghalf[:, 0:TC], ALU.pow).then_inc(pool_done, 1)

        @block.scalar
        def _(act):
            with act.Fori(0, NCH // 2) as i:
                for s in range(2):
                    ch, t0 = 2 * i + s, TB * i + TC * s
                    act.wait_ge(pe_done, at(pe_done, ch, "T_AO"))
                    act.activation(aoT[:, :], c.ps[:, 0, :], ACT.Copy).then_inc(act_done, 1)
                    act.activation(yT[:, :], c.yT_all[:, bass.ds(CH * ch, CH)], ACT.Copy).then_inc(act_done, 1)
                    act.wait_ge(pool_done, at(pool_done, ch, "R2"))
                    for j in range(TC):
                        ins = act.activation(x2n[:, j, :], x2[:, j, :], ACT.Copy, scale=r2[:, j:j + 1])
                    ins.then_inc(act_done, 1)
                    act.wait_ge(pe_done, at(pe_done, ch, "T_XF"))
                    act.activation(xfT[:, :], c.ps[:, 4, :], ACT.Copy, scale=col(c, "n2_w")).then_inc(act_done, 1)
                    act.activation(c.xfT_all[:, bass.ds(ch * CH, CH)], c.ps[:, 4, :], ACT.Copy, scale=col(c, "n2_w")).then_inc(act_done, 1)

        @block.vector
        def _(dve):
            with dve.Fori(0, NCH // 2) as i:
                for s in range(2):
                    ch, t0 = 2 * i + s, TB * i + TC * s
                    per, links = 1 + TC, [0]

                    def link(ins):
                        links[0] += 1
                        ins.then_inc(chain, 1)
                        dve.wait_ge(chain, per * ch + links[0])

                    dve.wait_ge(pe_done, at(pe_done, ch, "WO"))
                    dve.wait_ge(act_done, 1 + len(AC) * ch)
                    dve.tensor_tensor(x2[:, :, MZ:D], c.ps[:, 2, :].rearrange("p (t d) -> p t d", d=D)[:, :, 0:MW],
                                      c.xn1_all[:, bass.ds(t0, TC), MZ:D], ALU.add).then_inc(dve_done, 1)
                    dve.wait_ge(pe_done, at(pe_done, ch, "RO"))
                    link(dve.tensor_tensor(base[:, :, :], c.ps[:, 3, :].rearrange("p (t d) -> p t d", d=D),
                                           c.x_all[:, bass.ds(t0, TC), :], ALU.add))
                    dve.wait_ge(dve_done, at(dve_done, ch, "X2"))
                    dve.wait_ge(pool_done, at(pool_done, ch, "X2"))
                    dve.tensor_tensor(c.x_all[:, bass.ds(t0, TC), :], base[:, :, :], x2[:, :, :], ALU.add).then_inc(dve_done, 1)
                    for j in range(TC):
                        link(dve.tensor_tensor_reduce(out=junk[:, :], in0=x2[:, j, :], in1=x2[:, j, :], scale=1.0, scalar=0.0,
                                                      op0=ALU.mult, op1=ALU.add, accum_out=ms[:, j:j + 1]))
                    dve.tensor_scalar(ms[:, :], ms[:, :], 1.0 / D, 1.1920929e-07, ALU.mult, ALU.add).then_inc(dve_done, 1)
                    dve.wait_ge(pe_done, at(pe_done, ch, "GATE"))
                    dve.tensor_copy(c.lg_all[:, bass.ds(t0, TC), :], c.ps[:, 5, 0:TC * E1].rearrange("p (t e) -> p t e", e=E1)).then_inc(dve_done, 1)

        @block.tensor
        def _(pe):
            def each(fn):
                for j in range(TC):
                    ins = fn(j)
                ins.then_inc(pe_done, 1)

            tile = lambda j: slice(j * P, (j + 1) * P)
            ident = tab(c, "ident")
            with pe.Fori(0, NCH // 2) as i:
                for s in range(2):
                    ch = 2 * i + s
                    pe.wait_ge(pool_done, at(pool_done, ch, "AO"))
                    each(lambda j: pe.transpose(c.ps[:, 0, tile(j)], aos[:, j, :], ident))
                    pe.wait_ge(act_done, at(act_done, ch, "AOT"))
                    each(lambda j: pe.matmul(c.ps[:, 2, j * D:j * D + MW], aoT[:, tile(j)], w_of(c, "f1_o"), start=True, stop=True))
                    pe.wait_ge(act_done, at(act_done, ch, "YT"))
                    each(lambda j: pe.matmul(c.ps[:, 3, tile(j)], yT[:, tile(j)], w_of(c, "a1_o"), start=True, stop=True))
                    pe.wait_ge(act_done, at(act_done, ch, "X2N"))
                    each(lambda j: pe.transpose(c.ps[:, 4, tile(j)], x2n[:, j, :], ident))
                    pe.wait_ge(act_done, at(act_done, ch, "XFT"))
                    each(lambda j: pe.matmul(c.ps[:, 5, j * E1:(j + 1) * E1], xfT[:, tile(j)], w_of(c, "f1_gate"), start=True, stop=True))
                    pe.wait_ge(dve_done, 1 + len(DV) * (ch + 1))
                    pe.wait_ge(act_done, 1 + len(AC) * (ch + 1))


def stage_gate(nc, c):
    ph = ExitStack()
    sb = lambda name, shape, dt=F32: ph.enter_context(nc.sbuf_tensor("g1_" + name, shape, dt))
    sem = lambda name: nc.alloc_semaphore("g1_" + name)
    lg, ex, cnt, cmp, sel = (sb(n, [P, NT, E1]) for n in ("lg", "ex", "cnt", "cmp", "sel"))
    good = sb("good", [P, NT, E1], mybir.dt.uint32)
    red = sb("red", [P, NT])
    inv = sb("inv", [P, NT])
    chain, lg_ready, ex_ready = sem("chain"), sem("lg_ready"), sem("ex_ready")
    with ph, nc.Block() as block:
        @block.scalar
        def _(act):
            act.wait_ge(lg_ready, 1)
            act.activation(ex[:, :, :], lg[:, :, :], ACT.Exp).then_inc(ex_ready, 1)

        @block.vector
        def _(dve):
            links = [0]

            def link(ins):
                links[0] += 1
                ins.then_inc(chain, 1)
                dve.wait_ge(chain, links[0])

            wide = lambda a: a.unsqueeze(2).to_broadcast([P, NT, E1])
            link(dve.memset(lg[:, :, :], 0.0))
            link(dve.tensor_tensor(good[:, :, :], c.lg_all[:, :, :], c.lg_all[:, :, :], ALU.is_equal))
            link(dve.copy_predicated(lg[:, :, :], good[:, :, :], c.lg_all[:, :, :]))
            link(dve.tensor_scalar(lg[:, :, :], lg[:, :, :], FMAX, -FMAX, ALU.min, ALU.max))
            link(dve.tensor_reduce(red[:, :], lg[:, :, :], AX_X, ALU.max))
            dve.tensor_tensor(lg[:, :, :], lg[:, :, :], wide(red[:, :]), ALU.subtract).then_inc(lg_ready, 1)
            dve.wait_ge(ex_ready, 1)
            link(dve.tensor_reduce(red[:, :], ex[:, :, :], AX_X, ALU.add))
            link(dve.reciprocal(inv[:, :], red[:, :]))
            link(dve.tensor_tensor(ex[:, :, :], ex[:, :, :], wide(inv[:, :]), ALU.mult))
            link(dve.memset(cnt[:, :, :], 0.0))
            for f in range(E1):
                one = lambda a, b: ex[:, :, f:f + 1].to_broadcast([P, NT, b - a])
                if f + 1 < E1:
                    a, b = f + 1, E1
                    link(dve.tensor_tensor(cmp[:, :, a:b], one(a, b), ex[:, :, a:b], ALU.is_ge))
                    link(dve.tensor_tensor(cnt[:, :, a:b], cnt[:, :, a:b], cmp[:, :, a:b], ALU.add))
                if f:
                    a, b = 0, f
                    link(dve.tensor_tensor(cmp[:, :, a:b], one(a, b), ex[:, :, a:b], ALU.is_gt))
                    link(dve.tensor_tensor(cnt[:, :, a:b], cnt[:, :, a:b], cmp[:, :, a:b], ALU.add))
            link(dve.scalar_tensor_tensor(out=sel[:, :, :], in0=cnt[:, :, :], scalar=2.0, in1=ex[:, :, :],
                                          op0=ALU.is_lt, op1=ALU.mult))
            link(dve.tensor_reduce(red[:, :], sel[:, :, :], AX_X, ALU.add))
            link(dve.tensor_scalar(red[:, :], red[:, :], 1e-8, None, ALU.add))
            link(dve.reciprocal(inv[:, :], red[:, :]))
            link(dve.tensor_tensor(c.wts_all[:, :, :], sel[:, :, :], wide(inv[:, :]), ALU.mult))


def stage_experts(nc, c):
    ph = ExitStack()
    sb = lambda name, shape, dt=F32: ph.enter_context(nc.sbuf_tensor("e_" + name, shape, dt))
    sem = lambda name: nc.alloc_semaphore("e_" + name)
    UPS = [("e2_l1", None, "l1"), ("e3_dn", None, "d3"), ("e0_up", None, "u0"), ("e2_l2", "l1", "l2"), ("e3_up", "d3", "u3"),
           ("e1_w1", None, "a1"), ("e2_l3", "l2", "l3"), ("e1_w2", None, "b1")]
    DOWNS = [("e0_dn", "u0", 0), ("e3_out", "u3", 3), ("e2_l4", "l3", 2), ("e1_dn", "g1", 1)]
    units = []
    for w, src, dst in UPS:
        for half in range(WAT[w][1] // P // (2 if w in ("e2_l2", "e2_l3") else 1)):
            units.append((w, src, dst, half))
    NU = len(units)
    RB = 6
    hid = {n: sb(n, [P, k, CH]) for n, k in (("l1", 2), ("d3", 1), ("u0", 2), ("l2", 2), ("u3", 2), ("a1", 2), ("l3", 2), ("g1", 2))}
    th = sb("th", [P, 2, CH])
    wts = sb("wts", [P, 2, TC, E1])
    acc = sb("acc", [P, 2, TC, D])
    up_done, up_taken = sem("up_done"), sem("up_taken")
    gated = sem("gated")
    th_ready = sem("th_ready")
    dn_done, dn_taken = sem("dn_done"), sem("dn_taken")
    acc_ready = sem("acc_ready")
    written = [sem("written0"), sem("written1")]
    first_of = {}
    for u, (w, src, dst, half) in enumerate(units):
        first_of.setdefault(dst, u)
    width = {n: hid[n].shape[1] if n in hid else 2 for n in first_of}
    NA = NU - 2

    with ph, nc.Block() as block:
        @block.tensor
        def _(pe):
            with pe.Fori(0, NCH // 2) as i:
                for s in range(2):
                    ch = 2 * i + s
                    rhs_x = c.xfT_all[:, bass.ds(ch * CH, CH)]
                    pe.wait_ge(gated, 1 + 2 * ch)
                    pe.wait_ge(up_taken, 1 + NA * ch)
                    for u, (w, src, dst, half) in enumerate(units):
                        if u >= RB:
                            v = u - RB
                            pe.wait_ge(up_taken, 1 + NA * ch + v + 1)
                        kh = [0] if src is None else list(range(width[src]))
                        if src is not None:
                            pe.wait_ge(up_taken, 1 + NA * ch + first_of[src] + width[src])
                        for x in kh:
                            cols = w_of(c, w)[:, (x * HID if w in ("e2_l2", "e2_l3") else 0) + half * P:][:, 0:P]
                            ins = pe.matmul(c.ps[:, u % RB, :], cols, rhs_x if src is None else hid[src][:, x, :],
                                            start=(x == kh[0]), stop=(x == kh[-1]))
                        ins.then_inc(up_done, 1)
                    for k, (w, src, e) in enumerate(DOWNS):
                        if src == "g1":
                            pe.wait_ge(gated, 1 + 2 * ch + 2)
                        pe.wait_ge(dn_taken, 4 * ch + k + 1)
                        if src == "l3":
                            pe.wait_ge(up_taken, 1 + NA * (ch + 1))
                        elif src != "g1":
                            pe.wait_ge(up_taken, 1 + NA * ch + first_of[src] + width[src])
                        for j in range(TC):
                            for x in range(2):
                                ins = pe.matmul(c.ps[:, 6 + k % 2, j * D:j * D + MW], hid[src][:, x, j * P:(j + 1) * P],
                                                w_of(c, w)[:, x * MW:(x + 1) * MW], start=(x == 0), stop=(x == 1))
                        ins.then_inc(dn_done, 1)

        @block.scalar
        def _(act):
            with act.Fori(0, NCH // 2) as i:
                for s in range(2):
                    ch = 2 * i + s
                    act.wait_ge(dn_done, 1 + 4 * ch)
                    act.wait_ge(gated, 1 + 2 * ch)
                    for u, (w, src, dst, half) in enumerate(units[:NA]):
                        act.wait_ge(up_done, NU * ch + u + 1)
                        if dst == "a1":
                            act.activation(th[:, half, :], c.ps[:, u % RB, :], ACT.Tanh, scale=0.5).then_inc(th_ready, 1)
                            act.activation(hid["a1"][:, half, :], c.ps[:, u % RB, :], ACT.Copy, scale=0.5).then_inc(up_taken, 1)
                        else:
                            act.activation(hid[dst][:, half, :], c.ps[:, u % RB, :], ACT.Gelu).then_inc(up_taken, 1)

        @block.gpsimd
        def _(pool):
            pool.sem_inc(dn_taken, 2)
            for ahead in (gated, up_taken, dn_done):
                pool.sem_inc(ahead, 1)
            for ahead in written:
                pool.sem_inc(ahead, 16)
            with pool.Fori(0, NCH // 2) as i:
                for s in range(2):
                    ch, t0 = 2 * i + s, TB * i + TC * s
                    pool.wait_ge(written[s], 16 + 16 * i)
                    pool.wait_ge(dn_taken, 2 + 4 * ch)
                    fixed(pool)
                    pool.tensor_copy(acc[:, s, :, :], c.x_all[:, bass.ds(t0, TC), :])
                    pool.tensor_copy(wts[:, s, :, :], c.wts_all[:, bass.ds(t0, TC), :]).then_inc(acc_ready, 1)

        @block.vector
        def _(dve):
            with dve.Fori(0, NCH // 2) as i:
                for s in range(2):
                    ch = 2 * i + s
                    a1, g1 = hid["a1"], hid["g1"]
                    f = first_of["a1"]
                    dve.wait_ge(up_taken, 1 + NA * ch + f + 2)
                    for half in range(2):
                        dve.scalar_tensor_tensor(out=a1[:, half, :], in0=th[:, half, :], scalar=1.0, in1=a1[:, half, :],
                                                 op0=ALU.add, op1=ALU.mult).then_inc(c.silu, 1)
                    dve.wait_ge(dn_done, 1 + 4 * ch)
                    for half in range(2):
                        dve.wait_ge(c.silu, 2 * ch + half + 1)
                        dve.wait_ge(up_done, NU * (ch + 1) - 1 + half)
                        dve.tensor_tensor(g1[:, half, :], c.ps[:, (NA + half) % RB, :], a1[:, half, :], ALU.mult).then_inc(gated, 1)
                    dve.wait_ge(acc_ready, ch + 1)
                    for k, (w, src, e) in enumerate(DOWNS):
                        dve.wait_ge(dn_done, 1 + 4 * ch + k + 1)
                        if k:
                            dve.wait_ge(dn_taken, 2 + 4 * ch + k)
                        for j in range(TC):
                            ins = dve.scalar_tensor_tensor(out=acc[:, s, j, MZ:D], in0=c.ps[:, 6 + k % 2, j * D:j * D + MW],
                                                           scalar=wts[:, s, j, e:e + 1], in1=acc[:, s, j, MZ:D], op0=ALU.mult, op1=ALU.add)
                        ins.then_inc(dn_taken, 1)

        @block.sync
        def _(sp):
            with sp.Fori(0, NCH // 2) as i:
                for s in range(2):
                    ch, t0 = 2 * i + s, TB * i + TC * s
                    sp.wait_ge(dn_taken, 2 + 4 * (ch + 1))
                    fixed(sp)
                    sp.dma_start(c.out.rearrange("(t p) d -> p t d", p=P)[:, bass.ds(t0, TC), :], acc[:, s, :, :]).then_inc(written[s], 16)
            for s in range(2):
                sp.wait_ge(written[s], 16 + 16 * (NCH // 2))


def build(nc, x, w, cols, tabs, out, debug=None):
    c = Ctx()
    c.in_x, c.in_w, c.in_cols, c.in_tab, c.out = x, w, cols, tabs, out
    c.scr_q = [nc.dram_tensor(f"scratch_q{k}", (P, 3, B * T), BF16, kind="Internal").ap() for k in range(2)]
    c.scr_k = [nc.dram_tensor(f"scratch_k{k}", (P, 3, B * T), BF16, kind="Internal").ap() for k in range(2)]
    c.pool_chain = nc.alloc_semaphore("pool_chain")
    Ctx.passed = nc.alloc_semaphore("passed")
    c.norm_link = nc.alloc_semaphore("norm_link")
    c.norms = 0
    c.silu = nc.alloc_semaphore("silu")
    with ExitStack() as ctx:
        sb = lambda name, shape, dt=F32: ctx.enter_context(nc.sbuf_tensor(name, shape, dt))
        c.w = sb("weights", [P, NW])
        c.cols = sb("columns", [P, len(COLS)])
        c.head_cols = c.cols[:, COLS.index("head0"):COLS.index("head0") + 2 * G]
        c.tab = sb("tables", [P, NTAB])
        c.x_all = sb("x_all", [P, NT, D])
        c.acc_all = sb("acc_all", [P, NT, D])
        c.v_all = sb("v_all", [P, N, TB, G * DH])
        c.ao_all = sb("ao_all", [P, N, TB, G * DH])
        c.xn1_all = c.acc_all
        c.yT_all = sb("yT_all", [P, B * T])
        c.gn_stats = sb("gn_stats", [P, NCH, 6])
        c.xfT_all = c.v_all[:, :, :, :].rearrange("p n t d -> p (n t d)")
        c.lg_all = sb("lg_all", [P, NT, E1])
        c.wts_all = sb("wts_all", [P, NT, E1])
        c.ident_bf = sb("ident_bf", [P, P], BF16)
        c.mask_bf = sb("mask_bf", [P, P], BF16)
        c.neghalf = sb("neghalf", [P, P])
        c.qm = sb("qm", [P, 2, 2 * T], BF16)
        c.km = sb("km", [P, 2, 2 * T], BF16)
        c.vst = sb("vst", [P, 2, TB * G, 32])
        c.ps = ctx.enter_context(nc.psum_tensor("banks", [P, 8, CH], F32))
        stage_setup(nc, c)
        stage_first(nc, c)
        stage_attention(nc, c, "a0_", c.scr_q[0], c.scr_k[0], c.v_all, c.ao_all)
        stage_between(nc, c)
        stage_attention(nc, c, "a1_", c.scr_q[1], c.scr_k[1], c.v_all, c.ao_all)
        stage_groupnorm(nc, c)
        stage_after(nc, c)
        stage_gate(nc, c)
        stage_experts(nc, c)
        if debug:
            debug(nc, c)


def layout(i):
    f = np.float32
    a = {k: np.asarray(v) for k, v in i.items()}
    t = lambda m: m.T
    two = lambda m: np.concatenate([m[:P], m[P:]], 1)
    L0, L1, F = "L0_attn_", "L1_attn_", "L1_ffn_"
    ws = {
        "a0_q": t(a[L0 + "Wq"]), "a0_k": t(a[L0 + "Wk"]), "a0_v": t(a[L0 + "Wv"]), "a0_o": t(a[L0 + "Wo"]),
        "f0_e": a["L0_ffn_expert_w"].transpose(1, 0, 2).reshape(D, E0 * D), "f0_gate": a["L0_ffn_gate_w"],
        "a1_q": t(a[L1 + "W_q"]), "a1_k": t(a[L1 + "W_k"]),
        "a1_kv": np.concatenate([t(a[L1 + "W_k"]), t(a[L1 + "W_v"])], 1), "a1_o": t(a[L1 + "W_o"]),
        "f1_qkv": np.concatenate([t(a[F + "wq"]), t(a[F + "wk"]), t(a[F + "wv"])], 1),
        "f1_o": t(a[F + "wo"])[:, MZ:], "f1_gate": t(a[F + "gate_w"]),
        "e0_up": t(a[F + "e0_up"]), "e0_dn": two(t(a[F + "e0_down"])[:, MZ:]),
        "e1_w1": t(a[F + "e1_w1"]), "e1_w2": t(a[F + "e1_w2"]), "e1_dn": two(t(a[F + "e1_down"])[:, MZ:]),
        "e2_l1": t(a[F + "e2_l1"]), "e2_l2": two(t(a[F + "e2_l2"])), "e2_l3": two(t(a[F + "e2_l3"])),
        "e2_l4": two(t(a[F + "e2_l4"])[:, MZ:]),
        "e3_dn": t(a[F + "e3_down"]), "e3_up": t(a[F + "e3_up"]), "e3_out": two(t(a[F + "e3_out"])[:, MZ:]),
    }
    w = np.concatenate([ws[n] for n, _ in WCOLS], 1)
    gam = np.repeat(1.0 - 2.0 ** (-5.0 - np.arange(H)), DH)
    pos = np.arange(P)
    cs = {"gn_w": a[L1 + "gn_weight"], "gn_b": a[L1 + "gn_bias"], "n1_w": a[F + "n1_w"], "n2_w": a[F + "n2_w"],
          "qn_w": np.tile(a[F + "qn_w"], H), "kn_w": np.tile(a[F + "kn_w"], H), "g128": (gam ** P).astype(f),
          **{f"head{k}": ((np.arange(D) // DH) % (2 * G) == k).astype(f) for k in range(2 * G)}}
    cols = np.stack([cs[n] for n in COLS], 1)
    same = (np.arange(D)[:, None] // DH) == (np.arange(D)[None, :] // DH)
    ts = {
        "ident": np.eye(P, dtype=f), "mask": np.triu(np.full((P, P), NEG, f), 1),
        "gq": (gam[:, None] ** pos[None] / np.sqrt(DH)).astype(f), "gk": (gam[:, None] ** -pos[None]).astype(f),
        "gktok": (gam[None] ** -pos[:, None]).astype(f), "carry": (same * (gam ** P)[:, None]).astype(f),
        "head_mean": (same / DH).astype(f), "tri": np.triu(np.ones((P, P), f)),
        "bo": np.repeat(a[L0 + "bo"][None], P, 0), "gate_b": np.repeat(a["L0_ffn_gate_b"][None], P, 0),
        "f0_b": np.concatenate([a["L0_ffn_expert_b"], np.zeros((P - E0, D), f)], 0),
    }
    tabs = np.concatenate([ts[n] for n, _ in TABS], 1)
    x = a["L0_attn_x"].reshape(B * T, D)
    return {"in_x": x, "in_w": w, "in_cols": cols, "in_tab": tabs}


def kernel(**inputs):
    from concourse import bacc
    from concourse.bass_utils import run_bass_kernel_spmd

    nc = bacc.Bacc("TRN2", target_bir_lowering=False, num_devices=1)
    arrays = {k: np.ascontiguousarray(v) for k, v in layout(inputs).items()}
    args = [nc.dram_tensor(k, v.shape, mybir.dt.from_np(v.dtype), kind="ExternalInput").ap() for k, v in arrays.items()]
    out = nc.dram_tensor("out_0", (B * T, D), F32, kind="ExternalOutput").ap()
    build(nc, *args, out)
    r = run_bass_kernel_spmd(nc, [arrays], core_ids=[0])
    return r.results[0]["out_0"].reshape(B, T, D)
```
